# Optimizing a Trainium2 kernel written in Bass

```python
import numpy as np
import jax
import jax.numpy as jnp

def _softmax(x, axis=-1):
    return jax.nn.softmax(x, axis=axis)

def _gelu(x):
    return jax.nn.gelu(x, approximate=True)

def _silu(x):
    return jax.nn.silu(x)

def _sigmoid(x):
    return jax.nn.sigmoid(x)

def _layernorm(x, axis=-1, eps=1e-05):
    m = jnp.mean(x, axis=axis, keepdims=True)
    v = jnp.var(x, axis=axis, keepdims=True)
    return (x - m) / jnp.sqrt(v + eps)

def _scatter_add(tgt, idx, src, axis=0):
    return tgt.at[idx].add(src)

def _segment_sum(src, seg, n):
    return jax.ops.segment_sum(src, seg, n)
kernel_name = 'mk_seq_preln_d1_jaxref_r8_4fbdae'

def setup_inputs(seed: int=0):
    np.random.seed(seed)
    _w = jnp.asarray

    def _L0_attn_setup():
        import jax, jax.numpy as jnp
        import numpy as np
        DIM = 128
        NHEAD = 16
        HEAD_DIM = DIM // NHEAD

        def _rotate_half(t):
            h = t.shape[-1] // 2
            return jnp.concatenate([-t[..., h:], t[..., :h]], axis=-1)
        key = jax.random.key(seed)
        ks = jax.random.split(key, 5)
        B, N = (4, 256)
        return {'x': jax.random.normal(ks[0], (B, N, DIM), dtype=jnp.float32), 'qkv_w': jax.random.normal(ks[1], (3 * DIM, DIM), dtype=jnp.float32) * 0.02, 'qkv_b': jax.random.normal(ks[2], (3 * DIM,), dtype=jnp.float32) * 0.02, 'proj_w': jax.random.normal(ks[3], (DIM, DIM), dtype=jnp.float32) * 0.02, 'proj_b': jax.random.normal(ks[4], (DIM,), dtype=jnp.float32) * 0.02}
    _L0_attn_in = _L0_attn_setup()

    def _L0_ffn_setup():
        import jax, jax.numpy as jnp
        import numpy as np
        B, S, H, E = (2, 1024, 128, 8)
        SCALE = 0.5
        key = jax.random.key(seed)
        k1, k2 = jax.random.split(key)
        x = jax.random.normal(k1, (B, S, H), dtype=jnp.float32)
        gate_w = jax.random.normal(k2, (E, H), dtype=jnp.float32) * 0.02
        coeff = SCALE * (1.0 + 0.05 * jnp.arange(E, dtype=jnp.float32))
        expert_w = coeff[:, None, None] * jnp.eye(H, dtype=jnp.float32)
        return {'x': x, 'gate_w': gate_w, 'expert_w': expert_w}
    _L0_ffn_in = _L0_ffn_setup()
    _d = {'L0_attn_x': _L0_attn_in['x'], 'L0_attn_qkv_w': _L0_attn_in['qkv_w'], 'L0_attn_qkv_b': _L0_attn_in['qkv_b'], 'L0_attn_proj_w': _L0_attn_in['proj_w'], 'L0_attn_proj_b': _L0_attn_in['proj_b'], 'L0_ffn_gate_w': _L0_ffn_in['gate_w'], 'L0_ffn_expert_w': _L0_ffn_in['expert_w']}
    _x0 = _d['L0_attn_x']
    _d['L0_attn_x'] = jax.random.normal(jax.random.fold_in(jax.random.key(seed), 1), (4, 1024, 128), dtype=_x0.dtype)
    del _x0
    return _d

def reference(L0_attn_x, L0_attn_qkv_w, L0_attn_qkv_b, L0_attn_proj_w, L0_attn_proj_b, L0_ffn_gate_w, L0_ffn_expert_w):

    def _L0_attn_ref(x, qkv_w, qkv_b, proj_w, proj_b):
        import jax, jax.numpy as jnp
        import numpy as np
        DIM = 128
        NHEAD = 16
        HEAD_DIM = DIM // NHEAD

        def _rotate_half(t):
            h = t.shape[-1] // 2
            return jnp.concatenate([-t[..., h:], t[..., :h]], axis=-1)
        B, N, D = x.shape
        H, hd = (NHEAD, HEAD_DIM)
        qkv = x @ qkv_w.T + qkv_b
        qkv = jnp.transpose(qkv.reshape(B, N, 3, H, hd), (2, 0, 3, 1, 4))
        q, k, v = (qkv[0], qkv[1], qkv[2])
        inv_freq = 1.0 / 10000.0 ** (jnp.arange(0, hd, 2, dtype=x.dtype) / hd)
        pos = jnp.arange(N, dtype=x.dtype)
        freqs = pos[:, None] * inv_freq[None, :]
        emb = jnp.concatenate([freqs, freqs], axis=-1)
        cos = jnp.cos(emb)[None, None, None]
        sin = jnp.sin(emb)[None, None, None]
        q = q * cos + _rotate_half(q) * sin
        k = k * cos + _rotate_half(k) * sin
        scale = hd ** (-0.5)
        attn = jnp.einsum('abhqd,abhkd->abhqk', q, k) * scale
        attn = jax.nn.softmax(attn, axis=-1)
        out = jnp.einsum('abhqk,bhkd->abhqd', attn, v)
        out = jnp.swapaxes(out, 1, 2).reshape(B, N, D)
        out = out @ proj_w.T + proj_b
        return out

    def _L0_ffn_ref(x, gate_w, expert_w):
        import jax, jax.numpy as jnp
        import numpy as np
        B, S, H, E = (2, 1024, 128, 8)
        SCALE = 0.5
        scores = jnp.einsum('bsh,eh->bse', x, gate_w)
        chosen = jnp.argmax(scores, axis=-1)
        onehot = jax.nn.one_hot(chosen, gate_w.shape[0], dtype=x.dtype)
        expert_out = jnp.einsum('bsh,efh->bsef', x, expert_w)
        return x + jnp.einsum('bsef,bse->bsf', expert_out, onehot)
    x = L0_attn_x
    x = x + _L0_attn_ref(_layernorm(x, axis=-1), L0_attn_qkv_w, L0_attn_qkv_b, L0_attn_proj_w, L0_attn_proj_b)
    x = x + _L0_ffn_ref(_layernorm(x, axis=-1), L0_ffn_gate_w, L0_ffn_expert_w)
    return x

_drawn_inputs = setup_inputs


def setup_inputs(seed=0):
    import zlib

    import numpy as np

    out = dict(_drawn_inputs(seed))
    spreads = {}
    factors = {'L0_attn_qkv_w': 8.0, 'L0_attn_qkv_b': 8.0, 'L0_attn_proj_w': 8.0, 'L0_attn_proj_b': 2.721}
    for name, (base, spread) in spreads.items():
        noise = np.random.default_rng([zlib.crc32(name.encode()), seed]).standard_normal(out[name].shape)
        drawn = base * np.exp(spread * noise) if base else spread * noise
        out[name] = jnp.asarray(drawn.astype(out[name].dtype))
    for name, factor in factors.items():
        out[name] = (out[name] * factor).astype(out[name].dtype)
    return out
```

```python
import concourse.bass as bass
from concourse import mybir
from contextlib import ExitStack

P = 128
B, N, D = 4, 1024, 128
H, HD = 16, 8
E = 8
TILES = B * N // P
TPB = N // P
HALF = 512
UT = HALF // P
HEADS = B * H
SCALE = float(HD) ** -0.5
EPS = 1e-5
VW = HD + 1

Q_PARTS = [0, 1, 2, 0, 1, 0]
K_PARTS = [0, 0, 0, 1, 1, 2]
SPLITS = 3
SROWS = len(Q_PARTS) * HD
CROWS = SROWS + SPLITS


STEPS = TPB
LAG_S = 5
LAG_V = 1
S_OFF = STEPS + LAG_S
V_OFF = S_OFF + STEPS + LAG_V
T_MSP = STEPS + 1
TURN_HEADS = 4
TURN = TURN_HEADS * STEPS
TURNS = HEADS // TURN_HEADS
MASK_V = 2


def layer_kernel(nc, x, qkv_w, qkv_b, proj_w, proj_b, gate_w, expert_w, ident_rot_c, cos_c, sin_c, rank_c, out, parts, flat):
    f32, bf16 = mybir.dt.float32, mybir.dt.bfloat16
    ALU, ACT, AX = mybir.AluOpType, mybir.ActivationFunctionType, mybir.AxisListType

    ctx = ExitStack()
    with ctx:
        def sb(name, shape, dt=f32):
            return ctx.enter_context(nc.sbuf_tensor(name, shape, dt))

        def pb(name, shape, dt=f32):
            return ctx.enter_context(nc.psum_tensor(name, shape, dt))

        def sem(name):
            return ctx.enter_context(nc.semaphore(name))

        x_sb = sb("x_sb", [P, TILES, D])
        v_all = sb("v_all", [P, TILES, H, VW])
        ident_rot = sb("ident_rot", [P, 2, P])
        ident = ident_rot[:, 0, :]
        ident_bf = sb("ident_bf", [P, P], bf16)
        cos_t = sb("cos_t", [P, N])
        sin_t = sb("sin_t", [P, N])
        w_nat = sb("w_nat", [P, 3, D])
        w_t = sb("w_t", [P, 5, P])
        b_cols = sb("b_cols", [P, 2])
        b_qk = sb("b_qk", [P, 2, 2])
        vb_row = sb("vb_row", [P, D])
        pb_row = sb("pb_row", [P, D])
        pw_nat = sb("pw_nat", [P, D])
        pw_t = sb("pw_t", [P, D])
        gw_nat = sb("gw_nat", [E, D])
        gw_t = sb("gw_t", [P, E])
        ew_nat = sb("ew_nat", [P, E, D])
        ew_t = sb("ew_t", [P, E, D])
        rank = sb("rank", [P, UT, E])
        eps_c = sb("eps_c", [P, 1])
        credit = sb("credit", [P, 8])
        bn6 = sb("bn6", [P, TILES, 6])
        mv = sb("mv", [P, TILES, 2])
        std = sb("std", [P, TILES])
        rstd = sb("rstd", [P, TILES])
        xn = sb("xn", [P, 2, UT, D])
        xn_t = sb("xn_t", [P, 2, HALF])
        rc = sb("rc", [P, 2, 2, HALF])
        rope = sb("rope", [P, 2, HALF])
        res1 = sb("res1", [P, 2, HALF])
        split_sb = sb("split_sb", [P, 2, SPLITS, HALF], bf16)
        q_st = sb("q_st", [P, 2, N], bf16)
        k_st = sb("k_st", [P, 2, N], bf16)
        prob = sb("prob", [P, 2, TPB, N])
        v_ring = sb("v_ring", [P, 2, TPB, VW])
        zeros = sb("zeros", [P, TPB])
        mx = sb("mx", [P, 2, TPB, 2])
        mneg = sb("mneg", [P, 2, TPB])
        mres = sb("mres", [P, 2, TPB])
        msp = sb("msp", [P, 2, SPLITS, TPB], bf16)
        ms_t = sb("ms_t", [SPLITS * TPB, 2, P], bf16)
        rden = sb("rden", [P, 2, TPB])
        o_sb = sb("o_sb", [P, 2, TPB, HD])
        at_g = sb("at_g", [P, 2, UT, D])
        a_t = sb("a_t", [P, 2, HALF])
        x1 = sb("x1", [P, 2, UT, D])
        z = sb("z", [P, 2, UT, D])
        z_t = sb("z_t", [P, 2, HALF])
        x1z = sb("x1z", [P, 2, UT, D])
        best = sb("best", [P, 2, UT])
        hit = sb("hit", [P, 2, UT, E])
        rnk = sb("rnk", [P, 2, UT, E])
        brnk = sb("brnk", [P, 2, UT])
        onehot = sb("onehot", [P, 2, UT, E])
        bn6t = sb("bn6t", [P, 2, UT, 6])
        mvt = sb("mvt", [P, 2, UT, 2])
        stdt = sb("stdt", [P, 2, UT])
        rstdt = sb("rstdt", [P, 2, UT])

        ze = prob[:, 0, :, :].rearrange("p a (b e d) -> p (a b) e d", e=E, d=D).rearrange("p (g t) e d -> p g t e d", g=2)
        y_all = prob[:, 1, 0:TILES * D // N, :].rearrange("p a (b d) -> p (a b) d", d=D)
        ze_t = prob[:, 1, TILES * D // N:TILES * D // N + 2, :].rearrange("p a (e d) -> p a e d", e=E)

        ps_nat = [pb(f"ps_nat{i}", [P, HALF]) for i in range(2)]
        ps_s = [pb(f"ps_s{i}", [P, 2 * HALF]) for i in range(2)]
        ps_o = pb("ps_o", [P, HALF])
        ps_m = pb("ps_m", [P, HALF])
        ps_mt = ps_m[0:SPLITS * TPB, 0:P // 2].bitcast(bf16)

        s_x, s_const, s_wqkv, s_wtail, s_ones = sem("x_loaded"), sem("consts_loaded"), sem("qkv_w_loaded"), sem("tail_w_loaded"), sem("ones_set")
        s_idbf, s_rows, s_eps = sem("ident_bf_made"), sem("tail_rows_loaded"), sem("eps_set")
        s_pgt_ps, s_pgt_sb, s_ewt_ps, s_ewt_sb = sem("pw_gw_t_in_psum"), sem("pw_gw_t_in_sbuf"), sem("ew_t_in_psum"), sem("ew_t_in_sbuf")
        s_wt_ps, s_wt_sb = sem("w_t_in_psum"), sem("w_t_in_sbuf")
        s_bn, s_mv, s_std, s_rstd = sem("bn_stats"), sem("mean_var"), sem("std"), sem("rstd")
        s_xn, s_xt_ps, s_xt_sb = sem("xn_made"), sem("xn_t_in_psum"), sem("xn_t_in_sbuf")
        s_qk_ps, s_v_ps, s_rc, s_v_sb = sem("qk_in_psum"), sem("v_in_psum"), sem("rotary_products"), sem("v_in_sbuf")
        s_rope, s_hi, s_res, s_mid, s_lo = sem("rope_made"), sem("high_part"), sem("first_residue"), sem("middle_part"), sem("low_part")
        s_parts = [sem("parts_stored_even"), sem("parts_stored_odd")]
        s_stack = [sem(f"stack_loaded{i}") for i in range(4)]
        s_nat, s_mx, s_neg, s_mh, s_mr, s_mm, s_msp = sem("max_scores_in_psum"), sem("max_taken"), sem("max_negated"), sem("max_high"), sem("max_residue"), sem("max_middle"), sem("max_split")
        s_mt_ps, s_mt_sb = sem("max_rows_in_psum"), sem("max_rows_in_sbuf")
        s_mrow = [sem("max_rows_placed_even"), sem("max_rows_placed_odd")]
        s_sc, s_exp, s_pv, s_vr, s_rd, s_on = sem("scores_in_psum"), sem("exp_done"), sem("pv_done"), sem("v_ring_filled"), sem("den_inverted"), sem("head_normalised")
        s_xb = sem("x_biased")
        t_at = [sem("attn_staged_even"), sem("attn_staged_odd")]
        t_at_ps, t_at_sb, t_y_ps = sem("attn_t_in_psum"), sem("attn_t_in_sbuf"), sem("proj_in_psum")
        t_x1, t_bn, t_mv, t_std, t_rstd, t_z = sem("x1_made"), sem("t_bn_stats"), sem("t_mean_var"), sem("t_std"), sem("t_rstd"), sem("z_made")
        t_zt_ps, t_zt_sb, t_g_ps = sem("z_t_in_psum"), sem("z_t_in_sbuf"), sem("gate_in_psum")
        t_hit, t_best, t_rnk, t_brnk, t_oh = sem("best_hit"), sem("best_score"), sem("ranked"), sem("best_rank"), sem("onehot_made")
        t_x1z, t_zeV, t_zeP, t_ze_ps, t_ze_sb, t_ye_ps, t_out = sem("x1_plus_z"), sem("masked_by_vector"), sem("masked_by_pool"), sem("masked_t_in_psum"), sem("masked_t_in_sbuf"), sem("experts_in_psum"), sem("out_made")
        s_flat = [sem("head_stored_even"), sem("head_stored_odd")]
        s_out = sem("out_stored")

        out_t = out.rearrange("b (t p) d -> p (b t) d", p=P)
        block = ctx.enter_context(nc.Block())

        def at(t, off, it):
            r, i = divmod(t - off, STEPS)
            inside = not isinstance(it, int) or 0 <= TURN_HEADS * it + r < HEADS
            return (it * TURN_HEADS + r, r, i) if inside else (None, r, i)

        def turns(eng, turn):
            turn(0, TURN)
            with eng.Fori(1, TURNS) as it:
                turn(it, TURN)
            turn(TURNS, V_OFF + STEPS + 2)

        def need(eng, semaphore, count):
            if not isinstance(count, int) or count > 0:
                eng.wait_ge(semaphore, count)

        UNITS = TILES // UT

        def units(eng, unit):
            with eng.Fori(0, UNITS // 2 - 1) as it:
                for g in range(2):
                    unit(it * 2 + g, g, True)
            unit(UNITS - 2, 0, True)
            unit(UNITS - 1, 1, False)


        @block.sync
        def _(sp):
            sp.dma_start(x_sb[:, :, :], x.rearrange("b (t p) d -> p (b t) d", p=P)).then_inc(s_x, 16)
            sp.dma_start(w_nat[:, :, :], qkv_w.rearrange("(c p) d -> p c d", p=P)).then_inc(s_wqkv, 16)
            sp.dma_start(b_cols[:, :], qkv_b[0:2 * D].rearrange("(c p) -> p c", p=P), allow_slow_non_contiguous=True).then_inc(s_wqkv, 16)
            sp.dma_start(ident_rot[:, :, :], ident_rot_c).then_inc(s_wqkv, 16)
            sp.dma_start(pw_nat[:, :], proj_w).then_inc(s_wtail, 16)
            sp.dma_start(gw_nat[:, :], gate_w).then_inc(s_wtail, 16)
            sp.dma_start(ew_nat[:, :, :], expert_w.rearrange("e f h -> f e h")).then_inc(s_wtail, 16)
            sp.dma_start(cos_t[:, :], cos_c).then_inc(s_const, 16)
            sp.dma_start(sin_t[:, :], sin_c).then_inc(s_const, 16)
            sp.dma_start(vb_row[:, :], qkv_b[2 * D:3 * D].rearrange("(a d) -> a d", a=1).broadcast_to((P, D))).then_inc(s_const, 16)
            sp.dma_start(pb_row[:, :], proj_b.rearrange("(a d) -> a d", a=1).broadcast_to((P, D))).then_inc(s_rows, 16)
            sp.dma_start(rank[:, :, :], rank_c).then_inc(s_rows, 16)

            def park(f, g, ahead):
                for qk in range(2):
                    sp.wait_ge(s_lo, f * 2 + qk + 1)
                    for s in range(SPLITS):
                        sp.dma_start(parts[qk, s, :, bass.ds(f * HALF, HALF)], split_sb[:, qk, s, :]).then_inc(s_parts[qk], 16)
            units(sp, park)
            for qk in range(2):
                sp.wait_ge(s_parts[qk], 16 * SPLITS * (UNITS + 1))

            def load_stack(n, slot):
                row, ring = 64 * (slot % 2), slot // 2
                for qk, stack, order in ((0, q_st, Q_PARTS), (1, k_st, K_PARTS)):
                    for blk, s in enumerate(order):
                        sp.dma_start(stack[row + blk * HD:row + (blk + 1) * HD, ring, :],
                                     parts[qk, s, bass.ds((n % H) * HD, HD), bass.ds((n // H) * N, N)]).then_inc(s_stack[slot], 16)

            sp.wait_ge(s_ones, 1)
            for n in range(TURN_HEADS - 1):
                load_stack(n, n)

            def feed(it, r):
                n = it * TURN_HEADS + r
                row, ring = 64 * (r % 2), r // 2
                sp.wait_ge(s_mt_sb, n + 1)
                for s in range(SPLITS):
                    sp.dma_start(q_st[row + SROWS + s:row + SROWS + s + 1, ring, :].rearrange("a (t q) -> a t q", q=P),
                                 ms_t[s * TPB:(s + 1) * TPB, r % 2, :]).then_inc(s_mrow[r % 2], 16)
                if not isinstance(n, int) or n + 3 < HEADS:
                    need(sp, s_sc, n * STEPS)
                    load_stack(n + 3, (r + 3) % TURN_HEADS)

            for r in range(TURN_HEADS):
                feed(0, r)
            with sp.Fori(1, TURNS - 1) as it:
                for r in range(TURN_HEADS):
                    feed(it, r)
            for r in range(TURN_HEADS):
                feed(TURNS - 1, r)

            for par in range(2):
                sp.wait_ge(s_flat[par], 16 * HEADS // 2)
            flat_t = flat.rearrange("n (r u) c -> (n r) (u c)", u=2).rearrange("(t p) d -> p t d", p=P)

            def stage(n, g):
                sp.dma_start(at_g[:, g, :, :], flat_t[:, bass.ds(n * UT, UT), :]).then_inc(t_at[g], 16)

            stage(0, 0)

            def store(n, g, ahead):
                if ahead:
                    need(sp, t_at_ps, n)
                    stage(n + 1, 1 - g)
                sp.wait_ge(t_out, n + 1)
                sp.dma_start(out_t[:, bass.ds(n * UT, UT), :], y_all[:, bass.ds(n * UT, UT), :]).then_inc(s_out, 16)
            units(sp, store)
            sp.wait_ge(s_out, 16 * UNITS)

        @block.gpsimd
        def _(pool):
            nc.gpsimd.memset(eps_c[:, :], EPS).then_inc(s_eps, 1)
            for qk in range(2):
                nc.gpsimd.memset(credit[:, qk:qk + 1], 0.0).then_inc(s_parts[qk], 16 * SPLITS)
            nc.gpsimd.memset(credit[:, 4:5], 0.0).then_inc(s_rope, 2)
            nc.gpsimd.memset(zeros[:, :], 0.0)
            nc.gpsimd.memset(k_st[:, :, :], 1.0)
            nc.gpsimd.memset(v_all[:, :, :, :], 1.0).then_inc(s_ones, 1)
            pool.wait_ge(s_wqkv, 48)
            nc.gpsimd.tensor_copy(ident_bf[:, :], ident).then_inc(s_idbf, 1)

            def residues(f, g, ahead):
                for qk in range(2):
                    n = f * 2 + qk
                    pool.wait_ge(s_rc, n + 1 + 2)
                    nc.gpsimd.tensor_tensor(rope[:, qk, :], rc[:, qk, 0, :], rc[:, qk, 1, :], ALU.add).then_inc(s_rope, 1)
                    pool.wait_ge(s_hi, n + 1)
                    nc.gpsimd.tensor_tensor(res1[:, qk, :], rope[:, qk, :], split_sb[:, qk, 0, :], ALU.subtract).then_inc(s_res, 1)
                    pool.wait_ge(s_mid, n + 1)
                    nc.gpsimd.tensor_tensor(split_sb[:, qk, 2, :], res1[:, qk, :], split_sb[:, qk, 1, :], ALU.subtract).then_inc(s_lo, 1)
            units(pool, residues)

            pool.wait_ge(s_v_sb, UNITS + 1)

            def values(n, p):
                need(pool, s_pv, n - 1)
                nc.gpsimd.tensor_copy(v_ring[:, p, :, :], v_all[:, bass.ds((n // H) * TPB, TPB), bass.ds(n % H, 1), :].rearrange("p t a w -> p t (a w)")).then_inc(s_vr, 1)

            def split_max(n, p):
                pool.wait_ge(s_neg, n + 1)
                need(pool, s_mt_ps, n - 1)
                nc.gpsimd.tensor_tensor(msp[:, p, 0, :], mneg[:, p, :], zeros[:, :], ALU.subtract).then_inc(s_mh, 1)
                pool.wait_ge(s_mh, n + 1)
                nc.gpsimd.tensor_tensor(mres[:, p, :], mneg[:, p, :], msp[:, p, 0, :], ALU.subtract).then_inc(s_mr, 1)
                pool.wait_ge(s_mr, n + 1)
                nc.gpsimd.tensor_tensor(msp[:, p, 1, :], mres[:, p, :], zeros[:, :], ALU.subtract).then_inc(s_mm, 1)
                pool.wait_ge(s_mm, n + 1)
                nc.gpsimd.tensor_tensor(msp[:, p, 2, :], mres[:, p, :], msp[:, p, 1, :], ALU.subtract).then_inc(s_msp, 1)

            for r in range(TURN_HEADS):
                split_max(r, r % 2)
                values(r, r % 2)
                if r == 0:
                    pool.wait_ge(s_rows, 32)
                    pool.wait_ge(s_xn, UNITS)
                    nc.gpsimd.tensor_tensor(x_sb[:, :, :], x_sb[:, :, :], pb_row[:, :].rearrange("p (a d) -> p a d", a=1).broadcast_to((P, TILES, D)), ALU.add).then_inc(s_xb, 1)
            with pool.Fori(1, TURNS) as it:
                for r in range(TURN_HEADS):
                    split_max(it * TURN_HEADS + r, r % 2)
                    values(it * TURN_HEADS + r, r % 2)

            def mask(n, g, ahead):
                pool.wait_ge(t_oh, n + 1)
                for t in range(MASK_V, UT):
                    nc.gpsimd.tensor_tensor(ze[:, g, t, :, :], z[:, g, t:t + 1, :].broadcast_to((P, E, D)),
                                            onehot[:, g, t, :].rearrange("p (e a) -> p e a", a=1).broadcast_to((P, E, D)), ALU.mult).then_inc(t_zeP, 1)
                nc.gpsimd.tensor_tensor(x1z[:, g, :, :], x1[:, g, :, :], z[:, g, :, :], ALU.add).then_inc(t_x1z, 1)

            pool.wait_ge(s_on, HEADS)
            units(pool, mask)

        @block.scalar
        def _(act):
            act.wait_ge(s_ewt_ps, 1)
            nc.scalar.activation(ew_t[:, :, :].rearrange("p e d -> p (e d)"), ps_s[0][:, :], ACT.Copy).then_inc(s_ewt_sb, 1)
            act.wait_ge(s_eps, 1)
            act.wait_ge(s_mv, TILES)
            nc.scalar.activation(std[:, :], mv[:, :, 1], ACT.Sqrt, bias=eps_c[:, :]).then_inc(s_std, 1)

            def xt_copy(f, g):
                act.wait_ge(s_xt_ps, f + 1)
                nc.scalar.activation(xn_t[:, g, :], ps_m[:, :], ACT.Copy).then_inc(s_xt_sb, 1)

            def high_middle(f, g, ahead):
                for qk in range(2):
                    n = f * 2 + qk
                    act.wait_ge(s_rope, n + 1 + 2)
                    act.wait_ge(s_parts[qk], 16 * SPLITS * (f + 1))
                    nc.scalar.activation(split_sb[:, qk, 0, :], rope[:, qk, :], ACT.Copy).then_inc(s_hi, 1)
                    act.wait_ge(s_res, n + 1)
                    nc.scalar.activation(split_sb[:, qk, 1, :], res1[:, qk, :], ACT.Copy).then_inc(s_mid, 1)
                    if ahead and qk == 0:
                        xt_copy(f + 1, 1 - g)
            xt_copy(0, 0)
            units(act, high_middle)

            def turn(it, steps):
                for t in range(steps):
                    n, r, i = at(t, S_OFF, it)
                    if n is not None:
                        if i == 0:
                            need(act, s_pv, n - 1)
                        act.wait_ge(s_sc, n * STEPS + i + 1)
                        nc.scalar.activation(prob[:, r % 2, i, :], ps_s[i % 2][:, :], ACT.Exp, scale=SCALE).then_inc(s_exp, 1)
                    n, r, i = at(t, T_MSP, it)
                    if n is not None and i == 0:
                        act.wait_ge(s_mt_ps, n + 1)
                        need(act, s_mrow[r % 2], 16 * SPLITS * (it * 2 + r // 2))
                        nc.scalar.activation(ms_t[:, r % 2, :], ps_mt, ACT.Copy).then_inc(s_mt_sb, 1)
                    n, r, i = at(t, V_OFF + STEPS + 1, it)
                    if n is not None and i == 0:
                        act.wait_ge(s_on, n + 1)
                        act.dma_start(flat[bass.ds((n % H) * B + n // H, 1), :, :].rearrange("a p c -> p (a c)"),
                                      o_sb[:, r % 2, :, :].rearrange("p i d -> p (i d)")).then_inc(s_flat[r % 2], 16)
            turns(act, turn)

            def attn_copy(n, g):
                act.wait_ge(t_at_ps, n + 1)
                nc.scalar.activation(a_t[:, g, :], ps_m[:, :], ACT.Copy).then_inc(t_at_sb, 1)

            def root(n, g):
                act.wait_ge(t_mv, n * UT + UT)
                nc.scalar.activation(stdt[:, g, :], mvt[:, g, :, 1], ACT.Sqrt, bias=eps_c[:, :]).then_inc(t_std, 1)

            def z_copy(n, g):
                act.wait_ge(t_zt_ps, n + 1)
                nc.scalar.activation(z_t[:, g, :], ps_m[:, :], ACT.Copy).then_inc(t_zt_sb, 1)

            def masked_copy(n, t):
                act.wait_ge(t_ze_ps, n * UT + t + 1)
                nc.scalar.activation(ze_t[:, t % 2, :, :].rearrange("p e d -> p (e d)"), ps_s[t % 2][:, :], ACT.Copy).then_inc(t_ze_sb, 1)

            def tail_copies(n, g, ahead):
                masked_copy(n, 0)
                if ahead:
                    attn_copy(n + 1, 1 - g)
                masked_copy(n, 1)
                if ahead:
                    root(n + 1, 1 - g)
                masked_copy(n, 2)
                if ahead:
                    z_copy(n + 1, 1 - g)
                masked_copy(n, 3)
            attn_copy(0, 0)
            root(0, 0)
            z_copy(0, 0)
            units(act, tail_copies)

        @block.vector
        def _(dve):
            nc.vector.memset(credit[:, 2:3], 0.0).then_inc(s_rc, 2)
            nc.vector.memset(credit[:, 3:4], 0.0).then_inc(s_v_sb, 1)
            dve.wait_ge(s_wt_ps, 1)
            nc.vector.tensor_copy(w_t[:, 0:4, :].rearrange("p c d -> p (c d)"), ps_nat[0][:, :])
            nc.vector.tensor_copy(w_t[:, 4, :], ps_nat[1][:, 0:P])
            nc.vector.tensor_copy(b_qk[:, :, :].rearrange("p a b -> p (a b)"), ps_nat[1][:, P:P + 4]).then_inc(s_wt_sb, 1)
            dve.wait_ge(s_pgt_ps, 1)
            nc.vector.tensor_copy(pw_t[:, :], ps_nat[1][:, 2 * P:3 * P])
            nc.vector.tensor_copy(gw_t[:, :], ps_nat[1][:, 3 * P:3 * P + E]).then_inc(s_pgt_sb, 1)

            dve.wait_ge(s_x, 16)
            with dve.Fori(0, UNITS) as it:
                for t in range(UT):
                    nc.vector.bn_stats(bn6[:, bass.ds(it * UT + t, 1), :].rearrange("p a s -> p (a s)"), x_sb[:, bass.ds(it * UT + t, 1), :].rearrange("p a d -> p (a d)")).then_inc(s_bn, 1)
            dve.wait_ge(s_bn, TILES)
            for t in range(TILES):
                nc.vector.bn_aggr(mv[:, t, :], bn6[:, t, :]).then_inc(s_mv, 1)
            dve.wait_ge(s_std, 1)
            nc.vector.reciprocal(rstd[:, :], std[:, :]).then_inc(s_rstd, 1)
            dve.wait_ge(s_rstd, 1)
            dve.wait_ge(s_const, 48)

            def normalise(f, g):
                for t in range(UT):
                    c = f * UT + t
                    ins = nc.vector.tensor_scalar(xn[:, g, t, :], x_sb[:, bass.ds(c, 1), :].rearrange("p a d -> p (a d)"),
                                                  mv[:, bass.ds(c, 1), 0:1].rearrange("p a s -> p (a s)"), rstd[:, bass.ds(c, 1)], ALU.subtract, ALU.mult)
                ins.then_inc(s_xn, 1)

            def rotate(f, g, ahead):
                if ahead:
                    normalise(f + 1, 1 - g)
                for qk in range(2):
                    n = f * 2 + qk
                    dve.wait_ge(s_qk_ps, n + 1)
                    dve.wait_ge(s_rope, n + 1)
                    for a, table in ((0, cos_t), (1, sin_t)):
                        to = rc[:, qk, a, :] if qk else rc[:, qk, a, :].rearrange("p (i j) -> p j i", i=TPB)
                        src, tab = ps_s[qk][:, a * HALF:(a + 1) * HALF], table[:, g * HALF:(g + 1) * HALF]
                        if not qk:
                            src, tab = src.rearrange("p (j i) -> p j i", i=TPB), tab.rearrange("p (j i) -> p j i", i=TPB)
                        ins = nc.vector.scalar_tensor_tensor(to, src, b_qk[:, a, qk:qk + 1], tab, ALU.add, ALU.mult)
                    ins.then_inc(s_rc, 1)
                dve.wait_ge(s_v_ps, f + 1)
                nc.vector.tensor_tensor(v_all[:, bass.ds(f * UT, UT), :, 0:HD], ps_o[:, :].rearrange("p (t h w) -> p t h w", t=UT, h=H),
                                        vb_row[:, :].rearrange("p (a h w) -> p a h w", a=1, h=H).broadcast_to((P, UT, H, HD)), ALU.add).then_inc(s_v_sb, 1)
            dve.wait_ge(s_ones, 1)
            normalise(0, 0)
            units(dve, rotate)

            def turn(it, steps):
                for t in range(steps):
                    n, r, i = at(t, 0, it)
                    if n is not None:
                        if i == 0:
                            need(dve, s_neg, n - 1)
                        for half in range(2):
                            dve.wait_ge(s_nat, (n * STEPS + i) * 2 + half + 1)
                            nc.vector.tensor_reduce(mx[:, r % 2, i, half:half + 1], ps_nat[half][:, :], AX.X, ALU.max).then_inc(s_mx, 1)
                        if i == STEPS - 1:
                            dve.wait_ge(s_mx, (n + 1) * STEPS * 2)
                            need(dve, s_msp, n - 1)
                            nc.vector.tensor_reduce(mneg[:, r % 2, :], mx[:, r % 2, :, :], AX.X, ALU.max, negate=True).then_inc(s_neg, 1)
                    n, r, i = at(t, V_OFF + STEPS, it)
                    if n is not None and i == 0:
                        o = ps_o[:, 0:TPB * VW].rearrange("p (t w) -> p t w", w=VW)
                        dve.wait_ge(s_pv, n + 1)
                        nc.vector.reciprocal(rden[:, r % 2, :], o[:, :, HD]).then_inc(s_rd, 1)
                        dve.wait_ge(s_rd, n + 1)
                        need(dve, s_flat[r % 2], 16 * (it * 2 + r // 2))
                        nc.vector.tensor_tensor(o_sb[:, r % 2, :, :], o[:, :, 0:HD],
                                                rden[:, r % 2, :].rearrange("p (t a) -> p t a", a=1).broadcast_to((P, TPB, HD)), ALU.mult).then_inc(s_on, 1)
            turns(dve, turn)

            def second_norm(n, g):
                dve.wait_ge(t_y_ps, n + 1)
                nc.vector.tensor_tensor(x1[:, g, :, :], ps_o[:, :].rearrange("p (t d) -> p t d", t=UT), x_sb[:, bass.ds(n * UT, UT), :], ALU.add).then_inc(t_x1, 1)
                dve.wait_ge(t_x1, n + 1)
                for t in range(UT):
                    nc.vector.bn_stats(bn6t[:, g, t, :], x1[:, g, t, :]).then_inc(t_bn, 1)
                dve.wait_ge(t_bn, n * UT + UT)
                nc.vector.memset(credit[:, 5:6], 0.0)
                for t in range(UT):
                    nc.vector.bn_aggr(mvt[:, g, t, :], bn6t[:, g, t, :]).then_inc(t_mv, 1)
                dve.wait_ge(t_std, n + 1)
                nc.vector.reciprocal(rstdt[:, g, :], stdt[:, g, :]).then_inc(t_rstd, 1)
                dve.wait_ge(t_rstd, n + 1)
                for t in range(UT):
                    ins = nc.vector.tensor_scalar(z[:, g, t, :], x1[:, g, t, :], mvt[:, g, t, 0:1], rstdt[:, g, t:t + 1], ALU.subtract, ALU.mult)
                ins.then_inc(t_z, 1)

            def choose(n, g):
                gate = ps_m[:, 0:UT * E].rearrange("p (t e) -> p t e", e=E)
                over = (P, UT, E)
                dve.wait_ge(t_g_ps, n + 1)
                nc.vector.tensor_reduce(best[:, g, :], gate, AX.X, ALU.max).then_inc(t_best, 1)
                dve.wait_ge(t_best, n + 1)
                nc.vector.tensor_tensor(hit[:, g, :, :], gate, best[:, g, :].rearrange("p (t a) -> p t a", a=1).broadcast_to(over), ALU.is_equal).then_inc(t_hit, 1)
                dve.wait_ge(t_hit, n + 1)
                nc.vector.tensor_tensor(rnk[:, g, :, :], hit[:, g, :, :], rank[:, :, :], ALU.mult).then_inc(t_rnk, 1)
                dve.wait_ge(t_rnk, n + 1)
                nc.vector.tensor_reduce(brnk[:, g, :], rnk[:, g, :, :], AX.X, ALU.max).then_inc(t_brnk, 1)
                dve.wait_ge(t_brnk, n + 1)
                nc.vector.tensor_tensor(onehot[:, g, :, :], rnk[:, g, :, :], brnk[:, g, :].rearrange("p (t a) -> p t a", a=1).broadcast_to(over), ALU.is_equal).then_inc(t_oh, 1)

            def experts_in_out(n, g, ahead):
                dve.wait_ge(t_oh, n + 1)
                for t in range(MASK_V):
                    nc.vector.tensor_tensor(ze[:, g, t, :, :], z[:, g, t:t + 1, :].broadcast_to((P, E, D)),
                                            onehot[:, g, t, :].rearrange("p (e a) -> p e a", a=1).broadcast_to((P, E, D)), ALU.mult).then_inc(t_zeV, 1)
                if ahead:
                    second_norm(n + 1, 1 - g)
                    choose(n + 1, 1 - g)
                dve.wait_ge(t_ye_ps, n + 1)
                dve.wait_ge(t_x1z, n + 1)
                nc.vector.tensor_tensor(y_all[:, bass.ds(n * UT, UT), :], ps_nat[g][:, :].rearrange("p (t d) -> p t d", t=UT), x1z[:, g, :, :], ALU.add).then_inc(t_out, 1)
            dve.wait_ge(s_rows, 32)
            dve.wait_ge(s_xb, 1)
            second_norm(0, 0)
            choose(0, 0)
            units(dve, experts_in_out)

        @block.tensor
        def _(pe):
            mm = nc.tensor.matmul
            pe.wait_ge(s_wqkv, 48)
            id_rot = ident_rot[:, :, :].rearrange("p a f -> p (a f)")
            for qk in range(2):
                mm(ps_nat[0][:, qk * 2 * P:(qk + 1) * 2 * P], w_nat[:, qk, :], id_rot, start=True, stop=True)
            mm(ps_nat[1][:, 0:P], w_nat[:, 2, :], ident, start=True, stop=True)
            for a in range(2):
                ins = mm(ps_nat[1][:, P + 2 * a:P + 2 * a + 2], ident_rot[:, a, :], b_cols[:, :], start=True, stop=True)
            ins.then_inc(s_wt_ps, 1)
            pe.wait_ge(s_wtail, 48)
            pe.wait_ge(s_wt_sb, 1)
            nc.tensor.transpose(ps_nat[1][:, 2 * P:3 * P], pw_nat[:, :], ident)
            nc.tensor.transpose(ps_nat[1][:, 3 * P:3 * P + E], gw_nat[:, :], ident_rot[0:E, 0, 0:E]).then_inc(s_pgt_ps, 1)
            for e in range(E):
                ins = nc.tensor.transpose(ps_s[0][:, e * P:(e + 1) * P], ew_nat[:, e, :], ident)
            ins.then_inc(s_ewt_ps, 1)

            def tokens_t(f, g):
                pe.wait_ge(s_xn, f + 1)
                for t in range(UT):
                    ins = nc.tensor.transpose(ps_m[:, t * P:(t + 1) * P], xn[:, g, t, :], ident)
                ins.then_inc(s_xt_ps, 1)

            def project(f, g, ahead):
                pe.wait_ge(s_xt_sb, f + 1)
                for qk in range(2):
                    pe.wait_ge(s_rc, f * 2 + qk + 1)
                    for a in range(2):
                        ins = mm(ps_s[qk][:, a * HALF:(a + 1) * HALF], w_t[:, 2 * qk + a, :], xn_t[:, g, :], start=True, stop=True)
                    ins.then_inc(s_qk_ps, 1)
                    if ahead and qk == 0:
                        tokens_t(f + 1, 1 - g)
                pe.wait_ge(s_v_sb, f + 1)
                for t in range(UT):
                    ins = mm(ps_o[:, t * P:(t + 1) * P], xn_t[:, g, t * P:(t + 1) * P], w_t[:, 4, :], start=True, stop=True)
                ins.then_inc(s_v_ps, 1)
            tokens_t(0, 0)
            pe.wait_ge(s_ewt_sb, 1)
            pe.wait_ge(s_pgt_sb, 1)
            units(pe, project)
            pe.wait_ge(s_rc, 2 * UNITS + 2)
            pe.wait_ge(s_v_sb, UNITS + 1)
            pe.wait_ge(s_idbf, 1)

            q_by_i = q_st[:, :, :].rearrange("p a (u i j) -> p a i u j", u=2, i=TPB)

            def turn(it, steps):
                for t in range(steps):
                    nn, nr, ni = at(t, 0, it)
                    sn, sr, si = at(t, S_OFF, it)
                    for half in range(2):
                        cols = slice(half * HALF, (half + 1) * HALF)
                        if nn is not None:
                            row, ring = 64 * (nr % 2), nr // 2 % 2
                            if ni == 0 and half == 0:
                                pe.wait_ge(s_stack[nr % 4], 16 * 2 * len(Q_PARTS) * (it + nr // 4 + 1))
                            need(pe, s_mx, (nn * STEPS + ni) * 2 + half - 1)
                            mm(ps_nat[half][:, :], q_st[row:row + SROWS, ring, ni * P:(ni + 1) * P], k_st[row:row + SROWS, ring, cols],
                               start=True, stop=True).then_inc(s_nat, 1)
                        if sn is not None:
                            row, ring = 64 * (sr % 2), sr // 2 % 2
                            if si == 0 and half == 0:
                                pe.wait_ge(s_mrow[sr % 2], 16 * SPLITS * (it * 2 + sr // 2 + 1))
                            if half == 0:
                                need(pe, s_exp, sn * STEPS + si - 1)
                            ins = mm(ps_s[si % 2][:, cols], k_st[row:row + CROWS, ring, si * P:(si + 1) * P], q_by_i[row:row + CROWS, ring, half * TPB // 2:(half + 1) * TPB // 2, :, :],
                                     start=True, stop=True)
                    if sn is not None:
                        ins.then_inc(s_sc, 1)
                    n, r, i = at(t, V_OFF, it)
                    if n is not None:
                        if i == 0:
                            pe.wait_ge(s_exp, (n + 1) * STEPS)
                            pe.wait_ge(s_vr, n + 1)
                            need(pe, s_on, n)
                        for kt in range(TPB):
                            ins = mm(ps_o[:, i * VW:(i + 1) * VW], prob[:, r % 2, kt, i * P:(i + 1) * P], v_ring[:, r % 2, kt, :],
                                     start=kt == 0, stop=kt == TPB - 1)
                        if i == STEPS - 1:
                            ins.then_inc(s_pv, 1)
                    n, r, i = at(t, T_MSP, it)
                    if n is not None and i == 0:
                        pe.wait_ge(s_msp, n + 1)
                        need(pe, s_mt_sb, n)
                        nc.tensor.transpose(ps_mt, msp[:, r % 2, :, :].rearrange("p s t -> p (s t)"), ident_bf[:, :]).then_inc(s_mt_ps, 1)
            turns(pe, turn)

            def attn_proj(n, g):
                pe.wait_ge(t_at[g], 16 * ((n - g) // 2 + 1))
                for t in range(UT):
                    ins = nc.tensor.transpose(ps_m[:, t * P:(t + 1) * P], at_g[:, g, t, :], ident)
                ins.then_inc(t_at_ps, 1)
                pe.wait_ge(t_at_sb, n + 1)
                for t in range(UT):
                    ins = mm(ps_o[:, t * P:(t + 1) * P], a_t[:, g, t * P:(t + 1) * P], pw_t[:, :], start=True, stop=True)
                ins.then_inc(t_y_ps, 1)

            def gates(n, g):
                pe.wait_ge(t_z, n + 1)
                for t in range(UT):
                    ins = nc.tensor.transpose(ps_m[:, t * P:(t + 1) * P], z[:, g, t, :], ident)
                ins.then_inc(t_zt_ps, 1)
                pe.wait_ge(t_zt_sb, n + 1)
                for t in range(UT):
                    ins = mm(ps_m[:, t * E:(t + 1) * E], z_t[:, g, t * P:(t + 1) * P], gw_t[:, :], start=True, stop=True)
                ins.then_inc(t_g_ps, 1)

            def masked_t(n, g, t):
                if t < MASK_V:
                    pe.wait_ge(t_zeV, n * MASK_V + t + 1)
                else:
                    pe.wait_ge(t_zeP, n * (UT - MASK_V) + t - MASK_V + 1)
                for e in range(E):
                    ins = nc.tensor.transpose(ps_s[t % 2][:, e * P:(e + 1) * P], ze[:, g, t, e, :], ident)
                ins.then_inc(t_ze_ps, 1)

            def experts(n, g, t):
                pe.wait_ge(t_ze_sb, n * UT + t + 1)
                for e in range(E):
                    ins = mm(ps_nat[g][:, t * P:(t + 1) * P], ze_t[:, t % 2, e, :], ew_t[:, e, :], start=e == 0, stop=e == E - 1)
                if t == UT - 1:
                    ins.then_inc(t_ye_ps, 1)

            def tail_unit(n, g, ahead):
                masked_t(n, g, 0)
                if ahead:
                    attn_proj(n + 1, 1 - g)
                masked_t(n, g, 1)
                experts(n, g, 0)
                masked_t(n, g, 2)
                experts(n, g, 1)
                if ahead:
                    gates(n + 1, 1 - g)
                masked_t(n, g, 3)
                experts(n, g, 2)
                experts(n, g, 3)
            attn_proj(0, 0)
            gates(0, 0)
            units(pe, tail_unit)


_INS = ["L0_attn_x", "L0_attn_qkv_w", "L0_attn_qkv_b", "L0_attn_proj_w", "L0_attn_proj_b", "L0_ffn_gate_w", "L0_ffn_expert_w"]


def _constants():
    import numpy as np
    f = np.arange(P)
    id_rot = np.zeros((P, 2, P), np.float32)
    id_rot[f, 0, f] = 1.0
    low = f % HD < HD // 2
    id_rot[np.where(low, f + HD // 2, f - HD // 2), 1, f] = np.where(low, -1.0, 1.0)
    inv_freq = (np.float32(1.0) / np.float32(10000.0) ** (np.arange(0, HD, 2, dtype=np.float32) / np.float32(HD))).astype(np.float32)
    angle = np.arange(N, dtype=np.float32)[None, :] * inv_freq[f % (HD // 2)][:, None]
    rank = np.tile(np.arange(E, 0, -1, dtype=np.float32), (P, UT, 1))
    return {"ident_rot": id_rot, "cos": np.cos(angle, dtype=np.float32), "sin": np.sin(angle, dtype=np.float32), "rank": rank}


def kernel(**inputs):
    import numpy as _np
    import concourse.bacc as _bacc
    from concourse import mybir as _mybir
    from concourse.bass_utils import run_bass_kernel_spmd as _run

    nc = _bacc.Bacc("TRN2", target_bir_lowering=False, num_devices=1)
    arrays, args = {}, []
    for name in _INS:
        arrays[f"in_{name}"] = _np.ascontiguousarray(inputs[name])
    for name, a in _constants().items():
        arrays[f"const_{name}"] = _np.ascontiguousarray(a)
    for name, a in arrays.items():
        args.append(nc.dram_tensor(name, a.shape, _mybir.dt.float32, kind="ExternalInput").ap())
    out = nc.dram_tensor("out_0", (B, N, D), _mybir.dt.float32, kind="ExternalOutput").ap()
    parts = nc.dram_tensor("parts", (2, SPLITS, P, B * N), _mybir.dt.bfloat16).ap()
    flat = nc.dram_tensor("flat", (HEADS, P, TPB * HD), _mybir.dt.float32).ap()
    layer_kernel(nc, *args, out, parts, flat)
    r = _run(nc, [arrays], core_ids=[0])
    return r.results[0]["out_0"]
```

```python
import concourse.bass as bass
from concourse import mybir
from contextlib import ExitStack

P = 128
B, N, D = 4, 1024, 128
H, HD = 16, 8
E = 8
TILES = B * N // P
TPB = N // P
HALF = 512
UT = HALF // P
HEADS = B * H
SCALE = float(HD) ** -0.5
EPS = 1e-5
OR = HD + 1
CG = 32

Q_PARTS = [0, 1, 2, 0, 1, 0]
K_PARTS = [0, 0, 0, 1, 1, 2]
SPLITS = 3
SROWS = len(Q_PARTS) * HD
CROWS = SROWS + SPLITS

GROUPS_C = P // HD
HALF_R = HALF // GROUPS_C
BLOCK = N // GROUPS_C

QH = 4
QUADS = HEADS // QH
STEPS = 32
LAG_S = 4
LUMP = 4
S_OFF = STEPS + LAG_S
V_OFF = S_OFF + LUMP
T_DEN = V_OFF + STEPS + 3
T_MAX = STEPS + 1
SLOTS = 16
MASK_V = 2


def layer_kernel(nc, x, qkv_w, qkv_b, proj_w, proj_b, gate_w, expert_w, ident_rot_c, cos_c, sin_c, rank_c, out, parts, heads_t, rden_t):
    f32, bf16 = mybir.dt.float32, mybir.dt.bfloat16
    ALU, ACT, AX = mybir.AluOpType, mybir.ActivationFunctionType, mybir.AxisListType

    ctx = ExitStack()
    with ctx:
        def sb(name, shape, dt=f32):
            return ctx.enter_context(nc.sbuf_tensor(name, shape, dt))

        def pb(name, shape, dt=f32):
            return ctx.enter_context(nc.psum_tensor(name, shape, dt))

        def sem(name):
            return ctx.enter_context(nc.semaphore(name))

        x_sb = sb("x_sb", [P, TILES, D])
        v_all = sb("v_all", [P, TILES, D])
        ident_rot = sb("ident_rot", [P, 2, P])
        ident = ident_rot[:, 0, :]
        ident_bf = sb("ident_bf", [P, P], bf16)
        cos_t = sb("cos_t", [P, N])
        sin_t = sb("sin_t", [P, N])
        w_nat = sb("w_nat", [P, 3, D])
        w_t = sb("w_t", [P, 5, P])
        b_cols = sb("b_cols", [P, 2])
        b_qk = sb("b_qk", [P, 2, 2])
        vb_row = sb("vb_row", [P, D])
        pb_row = sb("pb_row", [P, D])
        pw_nat = sb("pw_nat", [P, D])
        pw_t = sb("pw_t", [P, D])
        gw_nat = sb("gw_nat", [E, D])
        gw_t = sb("gw_t", [P, E])
        ew_nat = sb("ew_nat", [P, E, D])
        ew_t = sb("ew_t", [P, E, D])
        rank = sb("rank", [P, UT, E])
        eps_c = sb("eps_c", [P, 1])
        credit = sb("credit", [P, 8])
        bn6 = sb("bn6", [P, TILES, 6])
        mv = sb("mv", [P, TILES, 2])
        std = sb("std", [P, TILES])
        rstd = sb("rstd", [P, TILES])
        xn = sb("xn", [P, 2, UT, D])
        xn_t = sb("xn_t", [P, 2, HALF])
        rc = sb("rc", [P, 2, 2, HALF])
        rope = sb("rope", [P, 2, HALF])
        res1 = sb("res1", [P, 2, HALF])
        split_sb = sb("split_sb", [P, 2, SPLITS, HALF], bf16)
        q_mx = sb("q_mx", [P, 4, N], bf16)
        k_mx = sb("k_mx", [P, 4, N], bf16)
        q_sc = sb("q_sc", [P, 4, N], bf16)
        k_sc = sb("k_sc", [P, 4, N], bf16)
        prob = sb("prob", [P, SLOTS, 2, HALF])
        v_ring = sb("v_ring", [P, 2, TPB, QH, CG])
        mx = sb("mx", [P, 2, QH, TPB, 2])
        mneg = sb("mneg", [P, 2, QH, TPB])
        mres = sb("mres", [P, 2, QH, TPB])
        zeros = sb("zeros", [P, QH, TPB])
        msp = sb("msp", [P, 2, QH, SPLITS, TPB], bf16)
        ms_t = sb("ms_t", [QH * SPLITS * TPB, 2, P], bf16)
        o_sb = sb("o_sb", [P, 2, HALF])
        den = sb("den", [QH * GROUPS_C, 2, BLOCK])
        rden = sb("rden", [QH * GROUPS_C, 2, BLOCK])
        a_raw, a_rden = rc[:, 0, :, :], rc[:, 1, :, :]
        a_t = rope
        x1 = res1[:, :, :].rearrange("p g (t d) -> p g t d", d=D)
        z = xn
        z_t = xn_t
        x1z = sb("x1z", [P, 2, UT, D])
        best = sb("best", [P, 2, UT])
        hit = sb("hit", [P, 2, UT, E])
        rnk = sb("rnk", [P, 2, UT, E])
        brnk = sb("brnk", [P, 2, UT])
        onehot = sb("onehot", [P, 2, UT, E])
        bn6t = sb("bn6t", [P, 2, UT, 6])
        mvt = sb("mvt", [P, 2, UT, 2])
        stdt = sb("stdt", [P, 2, UT])
        rstdt = sb("rstdt", [P, 2, UT])

        ze = prob[:, 0:8, :, :].rearrange("p (g t) a (b d) -> p g t (a b) d", g=2, d=D)
        y_all = prob[:, 8:12, :, :].rearrange("p s a (b d) -> p (s a b) d", d=D)
        ze_t = prob[:, 12:14, :, :].rearrange("p s a (b d) -> p s (a b) d", d=D)

        ps_nat = [pb(f"ps_nat{i}", [P, HALF]) for i in range(2)]
        ps_s = [pb(f"ps_s{i}", [P, 2 * HALF]) for i in range(2)]
        ps_o = pb("ps_o", [P, HALF])
        ps_m = pb("ps_m", [P, HALF])
        ps_mt = ps_m[0:QH * SPLITS * TPB, 0:P // 2].bitcast(bf16)

        s_x, s_const, s_wqkv, s_wtail, s_ones = sem("x_loaded"), sem("consts_loaded"), sem("qkv_w_loaded"), sem("tail_w_loaded"), sem("ones_set")
        s_idbf, s_rows, s_eps = sem("ident_bf_made"), sem("tail_rows_loaded"), sem("eps_set")
        s_pgt_ps, s_pgt_sb, s_ewt_ps, s_ewt_sb = sem("pw_gw_t_in_psum"), sem("pw_gw_t_in_sbuf"), sem("ew_t_in_psum"), sem("ew_t_in_sbuf")
        s_wt_ps, s_wt_sb = sem("w_t_in_psum"), sem("w_t_in_sbuf")
        s_bn, s_mv, s_std, s_rstd = sem("bn_stats"), sem("mean_var"), sem("std"), sem("rstd")
        s_xn, s_xt_ps, s_xt_sb = sem("xn_made"), sem("xn_t_in_psum"), sem("xn_t_in_sbuf")
        s_qk_ps, s_v_ps, s_rc, s_v_sb = sem("qk_in_psum"), sem("v_in_psum"), sem("rotary_products"), sem("v_in_sbuf")
        s_rope, s_hi, s_res, s_mid, s_lo = sem("rope_made"), sem("high_part"), sem("first_residue"), sem("middle_part"), sem("low_part")
        s_parts = [sem("parts_stored_even"), sem("parts_stored_odd")]
        s_mstack = [sem("max_stack_even"), sem("max_stack_odd")]
        s_sstack = [sem("score_stack_even"), sem("score_stack_odd")]
        s_nat, s_mx, s_neg, s_mh, s_mr, s_mm, s_msp = sem("max_scores_in_psum"), sem("max_taken"), sem("max_negated"), sem("max_high"), sem("max_residue"), sem("max_middle"), sem("max_split")
        s_mt_ps, s_mt_sb = sem("max_rows_in_psum"), sem("max_rows_in_sbuf")
        s_mrow = [sem("max_rows_placed_even"), sem("max_rows_placed_odd")]
        s_sc, s_exp, s_pv, s_vr, s_o = sem("scores_in_psum"), sem("exp_done"), sem("lump_done"), sem("v_ring_filled"), sem("half_in_sbuf")
        s_den, s_rd, s_rdst = sem("den_loaded"), sem("den_inverted"), sem("rden_stored")
        s_xb = sem("x_biased")
        t_at = [sem("attn_staged_even"), sem("attn_staged_odd")]
        t_an, t_y_ps = sem("attn_normalised"), sem("proj_in_psum")
        t_x1, t_bn, t_mv, t_std, t_rstd, t_z = sem("x1_made"), sem("t_bn_stats"), sem("t_mean_var"), sem("t_std"), sem("t_rstd"), sem("z_made")
        t_zt_ps, t_zt_sb, t_g_ps = sem("z_t_in_psum"), sem("z_t_in_sbuf"), sem("gate_in_psum")
        t_hit, t_best, t_rnk, t_brnk, t_oh = sem("best_hit"), sem("best_score"), sem("ranked"), sem("best_rank"), sem("onehot_made")
        t_x1z, t_zeV, t_zeP, t_ze_ps, t_ze_sb, t_ye_ps, t_out = sem("x1_plus_z"), sem("masked_by_vector"), sem("masked_by_pool"), sem("masked_t_in_psum"), sem("masked_t_in_sbuf"), sem("experts_in_psum"), sem("out_made")
        s_ost = [sem("first_half_stored"), sem("second_half_stored")]
        s_out = sem("out_stored")

        out_t = out.rearrange("b (t p) d -> p (b t) d", p=P)
        block = ctx.enter_context(nc.Block())

        def at(t, off, base, it):
            q, u = divmod(t - off, STEPS)
            if isinstance(base, int) and not 0 <= base + q < QUADS:
                return None, 0, 0, 0
            return base + q, q % 2, it + q // 2, u

        def turns(eng, turn, peel=1):
            turn(0, 0, 2 * peel * STEPS)
            with eng.Fori(peel, QUADS // 2) as it:
                turn(it * 2, it, 2 * STEPS)
            turn(QUADS, QUADS // 2, T_DEN + 1)

        def need(eng, semaphore, count):
            if not isinstance(count, int) or count > 0:
                eng.wait_ge(semaphore, count)

        UNITS = TILES // UT

        def units(eng, unit):
            with eng.Fori(0, UNITS // 2 - 1) as it:
                for g in range(2):
                    unit(it * 2 + g, g, True)
            unit(UNITS - 2, 0, True)
            unit(UNITS - 1, 1, False)


        @block.sync
        def _(sp):
            sp.dma_start(x_sb[:, :, :], x.rearrange("b (t p) d -> p (b t) d", p=P)).then_inc(s_x, 16)
            sp.dma_start(w_nat[:, :, :], qkv_w.rearrange("(c p) d -> p c d", p=P)).then_inc(s_wqkv, 16)
            sp.dma_start(b_cols[:, :], qkv_b[0:2 * D].rearrange("(c p) -> p c", p=P), allow_slow_non_contiguous=True).then_inc(s_wqkv, 16)
            sp.dma_start(ident_rot[:, :, :], ident_rot_c).then_inc(s_wqkv, 16)
            sp.dma_start(pw_nat[:, :], proj_w).then_inc(s_wtail, 16)
            sp.dma_start(gw_nat[:, :], gate_w).then_inc(s_wtail, 16)
            sp.dma_start(ew_nat[:, :, :], expert_w.rearrange("e f h -> f e h")).then_inc(s_wtail, 16)
            sp.dma_start(cos_t[:, :], cos_c).then_inc(s_const, 16)
            sp.dma_start(sin_t[:, :], sin_c).then_inc(s_const, 16)
            sp.dma_start(vb_row[:, :], qkv_b[2 * D:3 * D].rearrange("(a d) -> a d", a=1).broadcast_to((P, D))).then_inc(s_const, 16)
            sp.dma_start(pb_row[:, :], proj_b.rearrange("(a d) -> a d", a=1).broadcast_to((P, D))).then_inc(s_rows, 16)
            sp.dma_start(rank[:, :, :], rank_c).then_inc(s_rows, 16)

            def park(f, g, ahead):
                for qk in range(2):
                    sp.wait_ge(s_lo, f * 2 + qk + 1)
                    for s in range(SPLITS):
                        sp.dma_start(parts[qk, :, s, :, bass.ds(f * HALF, HALF)], split_sb[:, qk, s, :]).then_inc(s_parts[qk], 16)
            units(sp, park)
            for qk in range(2):
                sp.wait_ge(s_parts[qk], 16 * SPLITS * (UNITS + 1))

            def load_stacks(g, par, q_to, k_to, signal):
                for j in range(QH):
                    h = (g % (H // QH)) * QH + j
                    row, pair = 64 * (j % 2), par * 2 + j // 2
                    for s in range(SPLITS):
                        k = SPLITS - s
                        rows = slice(row + K_PARTS.index(s) * HD, row + (K_PARTS.index(s) + k) * HD)
                        col = bass.ds((g // (H // QH)) * N, N)
                        sp.dma_start(q_to[rows, pair, :], parts[0, bass.ds(h, 1), 0:k, :, col].rearrange("a s d n -> (a s d) n")).then_inc(signal, 16)
                        sp.dma_start(k_to[rows, pair, :], parts[1, bass.ds(h, 1), s, :, col].broadcast_to((k, HD, N))).then_inc(signal, 16)

            def store_half(g, half, k):
                sp.wait_ge(s_o, g * 2 + half + 1)
                for j in range(QH):
                    tok = ((g % (H // QH)) * QH + j) * (N // QH) + (g // (H // QH)) * BLOCK
                    sp.dma_start(heads_t[half * 8:(half + 1) * 8, :, bass.ds(tok, BLOCK)].rearrange("c o r -> o c r"),
                                 o_sb[j * CG:j * CG + OR, half, :].rearrange("o (c r) -> o c r", r=BLOCK)).then_inc(s_ost[half], 16)

            def feed(g, par, k, last=False):
                if not last:
                    need(sp, s_nat, g * STEPS * 2)
                    load_stacks(g + 1, 1 - par, q_mx, k_mx, s_mstack[1 - par])
                need(sp, s_sc, (g - 1) * STEPS)
                load_stacks(g, par, q_sc, k_sc, s_sstack[par])
                if not isinstance(g, int) or g > 0:
                    store_half(g - 1, 0, k)
                sp.wait_ge(s_mt_sb, g + 1)
                for j in range(QH):
                    row = 64 * (j % 2) + SROWS
                    for s in range(SPLITS):
                        src = (j * SPLITS + s) * TPB
                        sp.dma_start(q_sc[row + s:row + s + 1, par * 2 + j // 2, :].rearrange("a (t q) -> a t q", q=P),
                                     ms_t[src:src + TPB, par, :]).then_inc(s_mrow[par], 16)
                if not isinstance(g, int) or g > 0:
                    store_half(g - 1, 1, k)

            sp.wait_ge(s_ones, 1)
            load_stacks(0, 0, q_mx, k_mx, s_mstack[0])
            for g in range(2):
                feed(g, g, 0)
            with sp.Fori(1, QUADS // 2 - 1) as it:
                for g in range(2):
                    feed(it * 2 + g, g, it)
            for g in range(QUADS - 2, QUADS):
                feed(g, g % 2, 0, g == QUADS - 1)
            for half in range(2):
                store_half(QUADS - 1, half, 0)

            sp.wait_ge(s_rdst, 16 * QUADS)

            def stage(n, g):
                tok = bass.ds(n * HALF, HALF)
                sp.dma_start(a_raw[:, g, :], heads_t[:, 0:HD, tok]).then_inc(t_at[g], 16)
                sp.dma_start(a_rden[:, g, :], rden_t[:, tok].rearrange("c (a n) -> c a n", a=1).broadcast_to((GROUPS_C, HD, HALF))).then_inc(t_at[g], 16)

            stage(0, 0)

            def store(n, g, ahead):
                if ahead:
                    need(sp, t_an, n)
                    stage(n + 1, 1 - g)
                sp.wait_ge(t_out, n + 1)
                sp.dma_start(out_t[:, bass.ds(n * UT, UT), :], y_all[:, bass.ds(n * UT, UT), :]).then_inc(s_out, 16)
            units(sp, store)
            sp.wait_ge(s_out, 16 * UNITS)

        @block.gpsimd
        def _(pool):
            nc.gpsimd.memset(eps_c[:, :], EPS).then_inc(s_eps, 1)
            for qk in range(2):
                nc.gpsimd.memset(credit[:, qk:qk + 1], 0.0).then_inc(s_parts[qk], 16 * SPLITS)
            nc.gpsimd.memset(credit[:, 4:5], 0.0).then_inc(s_rope, 2)
            nc.gpsimd.memset(zeros[:, :, :], 0.0)
            nc.gpsimd.memset(v_ring[:, :, :, :, :], 1.0)
            nc.gpsimd.memset(k_sc[:, :, :], 1.0).then_inc(s_ones, 1)
            pool.wait_ge(s_wqkv, 48)
            nc.gpsimd.tensor_copy(ident_bf[:, :], ident).then_inc(s_idbf, 1)

            def residues(f, g, ahead):
                for qk in range(2):
                    n = f * 2 + qk
                    pool.wait_ge(s_rc, n + 1 + 2)
                    nc.gpsimd.tensor_tensor(rope[:, qk, :], rc[:, qk, 0, :], rc[:, qk, 1, :], ALU.add).then_inc(s_rope, 1)
                    pool.wait_ge(s_hi, n + 1)
                    nc.gpsimd.tensor_tensor(res1[:, qk, :], rope[:, qk, :], split_sb[:, qk, 0, :], ALU.subtract).then_inc(s_res, 1)
                    pool.wait_ge(s_mid, n + 1)
                    nc.gpsimd.tensor_tensor(split_sb[:, qk, 2, :], res1[:, qk, :], split_sb[:, qk, 1, :], ALU.subtract).then_inc(s_lo, 1)
            units(pool, residues)

            pool.wait_ge(s_v_sb, UNITS + 1)

            def values(g, p):
                need(pool, s_pv, (g - 1) * (STEPS // LUMP))
                nc.gpsimd.tensor_copy(v_ring[:, p, :, :, 0:HD], v_all[:, bass.ds((g // (H // QH)) * TPB, TPB), bass.ds((g % (H // QH)) * QH * HD, QH * HD)]
                                      .rearrange("p t (j d) -> p t j d", d=HD)).then_inc(s_vr, 1)

            def split_max(g, p):
                pool.wait_ge(s_neg, g + 1)
                need(pool, s_mt_ps, g - 1)
                nc.gpsimd.tensor_tensor(msp[:, p, :, 0, :], mneg[:, p, :, :], zeros[:, :, :], ALU.subtract).then_inc(s_mh, 1)
                pool.wait_ge(s_mh, g + 1)
                nc.gpsimd.tensor_tensor(mres[:, p, :, :], mneg[:, p, :, :], msp[:, p, :, 0, :], ALU.subtract).then_inc(s_mr, 1)
                pool.wait_ge(s_mr, g + 1)
                nc.gpsimd.tensor_tensor(msp[:, p, :, 1, :], mres[:, p, :, :], zeros[:, :, :], ALU.subtract).then_inc(s_mm, 1)
                pool.wait_ge(s_mm, g + 1)
                nc.gpsimd.tensor_tensor(msp[:, p, :, 2, :], mres[:, p, :, :], msp[:, p, :, 1, :], ALU.subtract).then_inc(s_msp, 1)

            def sums(g, p):
                cols = heads_t[:, HD, :].rearrange("c (j n) -> c j n", j=H)
                back = rden_t.rearrange("c (j n) -> c j n", j=H)
                where = (slice(None), bass.ds((g % (H // QH)) * QH, QH), bass.ds((g // (H // QH)) * BLOCK, BLOCK))
                for half in range(2):
                    pool.wait_ge(s_ost[half], 16 * QH * (g + 1))
                pool.dma_start(den[:, p, :], cols[where]).then_inc(s_den, 16)
                pool.wait_ge(s_rd, g + 1)
                pool.dma_start(back[where], rden[:, p, :]).then_inc(s_rdst, 16)

            def quad(g, p):
                values(g, p)
                split_max(g, p)
                if not isinstance(g, int) or g > 0:
                    sums(g - 1, 1 - p)

            quad(0, 0)
            pool.wait_ge(s_rows, 32)
            pool.wait_ge(s_xn, UNITS)
            nc.gpsimd.tensor_tensor(x_sb[:, :, :], x_sb[:, :, :], pb_row[:, :].rearrange("p (a d) -> p a d", a=1).broadcast_to((P, TILES, D)), ALU.add).then_inc(s_xb, 1)
            quad(1, 1)
            with pool.Fori(1, QUADS // 2) as it:
                for p in range(2):
                    quad(it * 2 + p, p)
            sums(QUADS - 1, 1)

            def mask(n, g, ahead):
                if ahead:
                    normalise(n + 1, 1 - g)
                pool.wait_ge(t_oh, n + 1)
                for t in range(MASK_V, UT):
                    nc.gpsimd.tensor_tensor(ze[:, g, t, :, :], z[:, g, t:t + 1, :].broadcast_to((P, E, D)),
                                            onehot[:, g, t, :].rearrange("p (e a) -> p e a", a=1).broadcast_to((P, E, D)), ALU.mult).then_inc(t_zeP, 1)
                nc.gpsimd.tensor_tensor(x1z[:, g, :, :], x1[:, g, :, :], z[:, g, :, :], ALU.add).then_inc(t_x1z, 1)

            def normalise(n, g):
                pool.wait_ge(t_at[g], 32 * ((n - g) // 2 + 1))
                nc.gpsimd.tensor_tensor(a_t[:, g, :], a_raw[:, g, :], a_rden[:, g, :], ALU.mult).then_inc(t_an, 1)

            normalise(0, 0)
            units(pool, mask)

        @block.scalar
        def _(act):
            act.wait_ge(s_ewt_ps, 1)
            nc.scalar.activation(ew_t[:, :, :].rearrange("p e d -> p (e d)"), ps_s[0][:, :], ACT.Copy).then_inc(s_ewt_sb, 1)
            act.wait_ge(s_eps, 1)
            act.wait_ge(s_mv, TILES)
            nc.scalar.activation(std[:, :], mv[:, :, 1], ACT.Sqrt, bias=eps_c[:, :]).then_inc(s_std, 1)

            def xt_copy(f, g):
                act.wait_ge(s_xt_ps, f + 1)
                nc.scalar.activation(xn_t[:, g, :], ps_m[:, :], ACT.Copy).then_inc(s_xt_sb, 1)

            def high_middle(f, g, ahead):
                for qk in range(2):
                    n = f * 2 + qk
                    act.wait_ge(s_rope, n + 1 + 2)
                    act.wait_ge(s_parts[qk], 16 * SPLITS * (f + 1))
                    nc.scalar.activation(split_sb[:, qk, 0, :], rope[:, qk, :], ACT.Copy).then_inc(s_hi, 1)
                    act.wait_ge(s_res, n + 1)
                    nc.scalar.activation(split_sb[:, qk, 1, :], res1[:, qk, :], ACT.Copy).then_inc(s_mid, 1)
                    if ahead and qk == 0:
                        xt_copy(f + 1, 1 - g)
            xt_copy(0, 0)
            units(act, high_middle)

            def turn(base, it, steps):
                for t in range(steps):
                    g, par, k, u = at(t, S_OFF, base, it)
                    if g is not None:
                        if u % LUMP == 0:
                            need(act, s_pv, g * (STEPS // LUMP) + u // LUMP - SLOTS // LUMP + 1)
                        act.wait_ge(s_sc, g * STEPS + u + 1)
                        nc.scalar.activation(prob[:, u % SLOTS, :, :].rearrange("p a q -> p (a q)"), ps_s[u % 2][:, :], ACT.Exp, scale=SCALE).then_inc(s_exp, 1)
                    g, par, k, u = at(t, T_MAX, base, it)
                    if g is not None and u == 0:
                        act.wait_ge(s_mt_ps, g + 1)
                        need(act, s_mrow[par], 16 * SPLITS * QH * k)
                        nc.scalar.activation(ms_t[:, par, :], ps_mt, ACT.Copy).then_inc(s_mt_sb, 1)
                    g, par, k, u = at(t, V_OFF + 1, base, it)
                    if g is not None and u % (STEPS // 2) == STEPS // 2 - LUMP:
                        half = u // (STEPS // 2)
                        act.wait_ge(s_pv, (g * 2 + half + 1) * (STEPS // 2 // LUMP))
                        need(act, s_ost[half], 16 * QH * g)
                        nc.scalar.activation(o_sb[:, half, :], ps_o[:, :], ACT.Copy).then_inc(s_o, 1)
            turns(act, turn)

            def root(n, g):
                act.wait_ge(t_mv, n * UT + UT)
                nc.scalar.activation(stdt[:, g, :], mvt[:, g, :, 1], ACT.Sqrt, bias=eps_c[:, :]).then_inc(t_std, 1)

            def z_copy(n, g):
                act.wait_ge(t_zt_ps, n + 1)
                nc.scalar.activation(z_t[:, g, :], ps_m[:, :], ACT.Copy).then_inc(t_zt_sb, 1)

            def masked_copy(n, t):
                act.wait_ge(t_ze_ps, n * UT + t + 1)
                nc.scalar.activation(ze_t[:, t % 2, :, :].rearrange("p e d -> p (e d)"), ps_s[t % 2][:, :], ACT.Copy).then_inc(t_ze_sb, 1)

            def tail_copies(n, g, ahead):
                masked_copy(n, 0)
                masked_copy(n, 1)
                if ahead:
                    root(n + 1, 1 - g)
                masked_copy(n, 2)
                if ahead:
                    z_copy(n + 1, 1 - g)
                masked_copy(n, 3)
            root(0, 0)
            z_copy(0, 0)
            units(act, tail_copies)

        @block.vector
        def _(dve):
            nc.vector.memset(credit[:, 2:3], 0.0).then_inc(s_rc, 2)
            nc.vector.memset(credit[:, 3:4], 0.0).then_inc(s_v_sb, 1)
            dve.wait_ge(s_wt_ps, 1)
            nc.vector.tensor_copy(w_t[:, 0:4, :].rearrange("p c d -> p (c d)"), ps_nat[0][:, :])
            nc.vector.tensor_copy(w_t[:, 4, :], ps_nat[1][:, 0:P])
            nc.vector.tensor_copy(b_qk[:, :, :].rearrange("p a b -> p (a b)"), ps_nat[1][:, P:P + 4]).then_inc(s_wt_sb, 1)
            dve.wait_ge(s_pgt_ps, 1)
            nc.vector.tensor_copy(pw_t[:, :], ps_nat[1][:, 2 * P:3 * P])
            nc.vector.tensor_copy(gw_t[:, :], ps_nat[1][:, 3 * P:3 * P + E]).then_inc(s_pgt_sb, 1)

            dve.wait_ge(s_x, 16)
            with dve.Fori(0, UNITS) as it:
                for t in range(UT):
                    nc.vector.bn_stats(bn6[:, bass.ds(it * UT + t, 1), :].rearrange("p a s -> p (a s)"), x_sb[:, bass.ds(it * UT + t, 1), :].rearrange("p a d -> p (a d)")).then_inc(s_bn, 1)
            dve.wait_ge(s_bn, TILES)
            for t in range(TILES):
                nc.vector.bn_aggr(mv[:, t, :], bn6[:, t, :]).then_inc(s_mv, 1)
            dve.wait_ge(s_std, 1)
            nc.vector.reciprocal(rstd[:, :], std[:, :]).then_inc(s_rstd, 1)
            dve.wait_ge(s_rstd, 1)
            dve.wait_ge(s_const, 48)

            def normalise(f, g):
                for t in range(UT):
                    c = f * UT + t
                    ins = nc.vector.tensor_scalar(xn[:, g, t, :], x_sb[:, bass.ds(c, 1), :].rearrange("p a d -> p (a d)"),
                                                  mv[:, bass.ds(c, 1), 0:1].rearrange("p a s -> p (a s)"), rstd[:, bass.ds(c, 1)], ALU.subtract, ALU.mult)
                ins.then_inc(s_xn, 1)

            def rotate(f, g, ahead):
                if ahead:
                    normalise(f + 1, 1 - g)
                for qk in range(2):
                    n = f * 2 + qk
                    dve.wait_ge(s_qk_ps, n + 1)
                    dve.wait_ge(s_rope, n + 1)
                    for a, table in ((0, cos_t), (1, sin_t)):
                        to = rc[:, qk, a, :] if qk else rc[:, qk, a, :].rearrange("p (c r) -> p r c", r=HALF_R)
                        src, tab = ps_s[qk][:, a * HALF:(a + 1) * HALF], table[:, g * HALF:(g + 1) * HALF]
                        if not qk:
                            src, tab = src.rearrange("p (r c) -> p r c", r=HALF_R), tab.rearrange("p (r c) -> p r c", r=HALF_R)
                        ins = nc.vector.scalar_tensor_tensor(to, src, b_qk[:, a, qk:qk + 1], tab, ALU.add, ALU.mult)
                    ins.then_inc(s_rc, 1)
                dve.wait_ge(s_v_ps, f + 1)
                nc.vector.tensor_tensor(v_all[:, bass.ds(f * UT, UT), :], ps_o[:, :].rearrange("p (t d) -> p t d", t=UT),
                                        vb_row[:, :].rearrange("p (a d) -> p a d", a=1).broadcast_to((P, UT, D)), ALU.add).then_inc(s_v_sb, 1)
            normalise(0, 0)
            units(dve, rotate)

            def turn(base, it, steps):
                for t in range(steps):
                    g, par, k, u = at(t, 0, base, it)
                    if g is not None:
                        if u == 0:
                            need(dve, s_neg, g - 1)
                        pair, half, tile = u % 2, u // 2 % 2, u // 4
                        for j in range(2):
                            dve.wait_ge(s_nat, (g * STEPS + u) * 2 + j + 1)
                            nc.vector.tensor_reduce(mx[:, par, pair * 2 + j, tile, half:half + 1], ps_nat[j][:, :], AX.X, ALU.max).then_inc(s_mx, 1)
                        if u == STEPS - 1:
                            dve.wait_ge(s_mx, (g + 1) * STEPS * 2)
                            need(dve, s_msp, g - 1)
                            nc.vector.tensor_reduce(mneg[:, par, :, :], mx[:, par, :, :, :], AX.X, ALU.max, negate=True).then_inc(s_neg, 1)
                    g, par, k, u = at(t, T_DEN, base, it)
                    if g is not None and u == 0:
                        dve.wait_ge(s_den, 16 * (g + 1))
                        need(dve, s_rdst, 16 * (g - 1))
                        nc.vector.reciprocal(rden[:, par, :], den[:, par, :]).then_inc(s_rd, 1)
            turns(dve, turn, 2)

            def second_norm(n, g):
                dve.wait_ge(t_y_ps, n + 1)
                nc.vector.tensor_tensor(x1[:, g, :, :], ps_o[:, :].rearrange("p (t d) -> p t d", t=UT), x_sb[:, bass.ds(n * UT, UT), :], ALU.add).then_inc(t_x1, 1)
                dve.wait_ge(t_x1, n + 1)
                for t in range(UT):
                    nc.vector.bn_stats(bn6t[:, g, t, :], x1[:, g, t, :]).then_inc(t_bn, 1)
                dve.wait_ge(t_bn, n * UT + UT)
                nc.vector.memset(credit[:, 5:6], 0.0)
                for t in range(UT):
                    nc.vector.bn_aggr(mvt[:, g, t, :], bn6t[:, g, t, :]).then_inc(t_mv, 1)
                dve.wait_ge(t_std, n + 1)
                nc.vector.reciprocal(rstdt[:, g, :], stdt[:, g, :]).then_inc(t_rstd, 1)
                dve.wait_ge(t_rstd, n + 1)
                for t in range(UT):
                    ins = nc.vector.tensor_scalar(z[:, g, t, :], x1[:, g, t, :], mvt[:, g, t, 0:1], rstdt[:, g, t:t + 1], ALU.subtract, ALU.mult)
                ins.then_inc(t_z, 1)

            def choose(n, g):
                gate = ps_m[:, 0:UT * E].rearrange("p (t e) -> p t e", e=E)
                over = (P, UT, E)
                dve.wait_ge(t_g_ps, n + 1)
                nc.vector.tensor_reduce(best[:, g, :], gate, AX.X, ALU.max).then_inc(t_best, 1)
                dve.wait_ge(t_best, n + 1)
                nc.vector.tensor_tensor(hit[:, g, :, :], gate, best[:, g, :].rearrange("p (t a) -> p t a", a=1).broadcast_to(over), ALU.is_equal).then_inc(t_hit, 1)
                dve.wait_ge(t_hit, n + 1)
                nc.vector.tensor_tensor(rnk[:, g, :, :], hit[:, g, :, :], rank[:, :, :], ALU.mult).then_inc(t_rnk, 1)
                dve.wait_ge(t_rnk, n + 1)
                nc.vector.tensor_reduce(brnk[:, g, :], rnk[:, g, :, :], AX.X, ALU.max).then_inc(t_brnk, 1)
                dve.wait_ge(t_brnk, n + 1)
                nc.vector.tensor_tensor(onehot[:, g, :, :], rnk[:, g, :, :], brnk[:, g, :].rearrange("p (t a) -> p t a", a=1).broadcast_to(over), ALU.is_equal).then_inc(t_oh, 1)

            def experts_in_out(n, g, ahead):
                dve.wait_ge(t_oh, n + 1)
                for t in range(MASK_V):
                    nc.vector.tensor_tensor(ze[:, g, t, :, :], z[:, g, t:t + 1, :].broadcast_to((P, E, D)),
                                            onehot[:, g, t, :].rearrange("p (e a) -> p e a", a=1).broadcast_to((P, E, D)), ALU.mult).then_inc(t_zeV, 1)
                if ahead:
                    second_norm(n + 1, 1 - g)
                    choose(n + 1, 1 - g)
                dve.wait_ge(t_ye_ps, n + 1)
                dve.wait_ge(t_x1z, n + 1)
                nc.vector.tensor_tensor(y_all[:, bass.ds(n * UT, UT), :], ps_nat[g][:, :].rearrange("p (t d) -> p t d", t=UT), x1z[:, g, :, :], ALU.add).then_inc(t_out, 1)
            dve.wait_ge(s_rows, 32)
            dve.wait_ge(s_xb, 1)
            second_norm(0, 0)
            choose(0, 0)
            units(dve, experts_in_out)

        @block.tensor
        def _(pe):
            mm = nc.tensor.matmul
            pe.wait_ge(s_wqkv, 48)
            id_rot = ident_rot[:, :, :].rearrange("p a f -> p (a f)")
            for qk in range(2):
                mm(ps_nat[0][:, qk * 2 * P:(qk + 1) * 2 * P], w_nat[:, qk, :], id_rot, start=True, stop=True)
            mm(ps_nat[1][:, 0:P], w_nat[:, 2, :], ident, start=True, stop=True)
            for a in range(2):
                ins = mm(ps_nat[1][:, P + 2 * a:P + 2 * a + 2], ident_rot[:, a, :], b_cols[:, :], start=True, stop=True)
            ins.then_inc(s_wt_ps, 1)
            pe.wait_ge(s_wtail, 48)
            pe.wait_ge(s_wt_sb, 1)
            nc.tensor.transpose(ps_nat[1][:, 2 * P:3 * P], pw_nat[:, :], ident)
            nc.tensor.transpose(ps_nat[1][:, 3 * P:3 * P + E], gw_nat[:, :], ident_rot[0:E, 0, 0:E]).then_inc(s_pgt_ps, 1)
            for e in range(E):
                ins = nc.tensor.transpose(ps_s[0][:, e * P:(e + 1) * P], ew_nat[:, e, :], ident)
            ins.then_inc(s_ewt_ps, 1)

            def tokens_t(f, g):
                pe.wait_ge(s_xn, f + 1)
                for t in range(UT):
                    ins = nc.tensor.transpose(ps_m[:, t * P:(t + 1) * P], xn[:, g, t, :], ident)
                ins.then_inc(s_xt_ps, 1)

            def project(f, g, ahead):
                pe.wait_ge(s_xt_sb, f + 1)
                for qk in range(2):
                    pe.wait_ge(s_rc, f * 2 + qk + 1)
                    for a in range(2):
                        ins = mm(ps_s[qk][:, a * HALF:(a + 1) * HALF], w_t[:, 2 * qk + a, :], xn_t[:, g, :], start=True, stop=True)
                    ins.then_inc(s_qk_ps, 1)
                    if ahead and qk == 0:
                        tokens_t(f + 1, 1 - g)
                pe.wait_ge(s_v_sb, f + 1)
                for t in range(UT):
                    ins = mm(ps_o[:, t * P:(t + 1) * P], xn_t[:, g, t * P:(t + 1) * P], w_t[:, 4, :], start=True, stop=True)
                ins.then_inc(s_v_ps, 1)
            tokens_t(0, 0)
            pe.wait_ge(s_ewt_sb, 1)
            pe.wait_ge(s_pgt_sb, 1)
            units(pe, project)
            pe.wait_ge(s_rc, 2 * UNITS + 2)
            pe.wait_ge(s_v_sb, UNITS + 1)
            pe.wait_ge(s_idbf, 1)

            q_by_c = q_sc[:, :, :].rearrange("p a (u c r) -> p a c u r", u=2, r=HALF_R)

            def turn(base, it, steps):
                for t in range(steps):
                    g, par, k, u = at(t, 0, base, it)
                    if g is not None:
                        pair, half, tile = u % 2, u // 2 % 2, u // 4
                        if u == 0:
                            pe.wait_ge(s_mstack[par], 16 * 2 * SPLITS * QH * (k + 1))
                        for j in range(2):
                            need(pe, s_mx, (g * STEPS + u) * 2 + j - 1)
                            rows = slice(64 * j, 64 * j + SROWS)
                            mm(ps_nat[j][:, :], q_mx[rows, par * 2 + pair, tile * P:(tile + 1) * P], k_mx[rows, par * 2 + pair, half * HALF:(half + 1) * HALF],
                               start=True, stop=True).then_inc(s_nat, 1)
                    g, par, k, u = at(t, S_OFF, base, it)
                    if g is not None:
                        pair, tile, half = u % 2, u // 2 % TPB, u // (2 * TPB)
                        if u == 0:
                            pe.wait_ge(s_sstack[par], 16 * 2 * SPLITS * QH * (k + 1))
                            pe.wait_ge(s_mrow[par], 16 * SPLITS * QH * (k + 1))
                        need(pe, s_exp, g * STEPS + u - 1)
                        for j in range(2):
                            rows = slice(64 * j, 64 * j + CROWS)
                            ins = mm(ps_s[u % 2][:, j * HALF:(j + 1) * HALF], k_sc[rows, par * 2 + pair, tile * P:(tile + 1) * P],
                                     q_by_c[rows, par * 2 + pair, half * 8:(half + 1) * 8, :, :], start=True, stop=True)
                        ins.then_inc(s_sc, 1)
                    g, par, k, u = at(t, V_OFF, base, it)
                    if g is not None and u % LUMP == 0:
                        half = u // (STEPS // 2)
                        if u == 0:
                            pe.wait_ge(s_vr, g + 1)
                        if u % (STEPS // 2) == 0:
                            need(pe, s_o, g * 2 + half)
                        pe.wait_ge(s_exp, g * STEPS + u + LUMP)
                        for tile in (u // 2 % TPB, u // 2 % TPB + 1):
                            for j in range(QH):
                                ins = mm(ps_o[j * CG:(j + 1) * CG, :], v_ring[:, par, tile, j, :], prob[:, tile * 2 + j // 2, j % 2, :],
                                         start=tile == 0, stop=tile == TPB - 1)
                        ins.then_inc(s_pv, 1)
                    g, par, k, u = at(t, T_MAX, base, it)
                    if g is not None and u == 0:
                        pe.wait_ge(s_msp, g + 1)
                        need(pe, s_mt_sb, g)
                        nc.tensor.transpose(ps_mt, msp[:, par, :, :, :].rearrange("p j s t -> p (j s t)"), ident_bf[:, :]).then_inc(s_mt_ps, 1)
            turns(pe, turn)

            def attn_proj(n, g):
                pe.wait_ge(t_an, n + 1)
                for t in range(UT):
                    ins = mm(ps_o[:, t * P:(t + 1) * P], a_t[:, g, t * P:(t + 1) * P], pw_t[:, :], start=True, stop=True)
                ins.then_inc(t_y_ps, 1)

            def gates(n, g):
                pe.wait_ge(t_z, n + 1)
                for t in range(UT):
                    ins = nc.tensor.transpose(ps_m[:, t * P:(t + 1) * P], z[:, g, t, :], ident)
                ins.then_inc(t_zt_ps, 1)
                pe.wait_ge(t_zt_sb, n + 1)
                for t in range(UT):
                    ins = mm(ps_m[:, t * E:(t + 1) * E], z_t[:, g, t * P:(t + 1) * P], gw_t[:, :], start=True, stop=True)
                ins.then_inc(t_g_ps, 1)

            def masked_t(n, g, t):
                if t < MASK_V:
                    pe.wait_ge(t_zeV, n * MASK_V + t + 1)
                else:
                    pe.wait_ge(t_zeP, n * (UT - MASK_V) + t - MASK_V + 1)
                for e in range(E):
                    ins = nc.tensor.transpose(ps_s[t % 2][:, e * P:(e + 1) * P], ze[:, g, t, e, :], ident)
                ins.then_inc(t_ze_ps, 1)

            def experts(n, g, t):
                pe.wait_ge(t_ze_sb, n * UT + t + 1)
                for e in range(E):
                    ins = mm(ps_nat[g][:, t * P:(t + 1) * P], ze_t[:, t % 2, e, :], ew_t[:, e, :], start=e == 0, stop=e == E - 1)
                if t == UT - 1:
                    ins.then_inc(t_ye_ps, 1)

            def tail_unit(n, g, ahead):
                masked_t(n, g, 0)
                if ahead:
                    attn_proj(n + 1, 1 - g)
                masked_t(n, g, 1)
                experts(n, g, 0)
                masked_t(n, g, 2)
                experts(n, g, 1)
                if ahead:
                    gates(n + 1, 1 - g)
                masked_t(n, g, 3)
                experts(n, g, 2)
                experts(n, g, 3)
            attn_proj(0, 0)
            gates(0, 0)
            units(pe, tail_unit)


_INS = ["L0_attn_x", "L0_attn_qkv_w", "L0_attn_qkv_b", "L0_attn_proj_w", "L0_attn_proj_b", "L0_ffn_gate_w", "L0_ffn_expert_w"]


def _constants():
    import numpy as np
    f = np.arange(P)
    id_rot = np.zeros((P, 2, P), np.float32)
    id_rot[f, 0, f] = 1.0
    low = f % HD < HD // 2
    id_rot[np.where(low, f + HD // 2, f - HD // 2), 1, f] = np.where(low, -1.0, 1.0)
    inv_freq = (np.float32(1.0) / np.float32(10000.0) ** (np.arange(0, HD, 2, dtype=np.float32) / np.float32(HD))).astype(np.float32)
    angle = np.arange(N, dtype=np.float32)[None, :] * inv_freq[f % (HD // 2)][:, None]
    rank = np.tile(np.arange(E, 0, -1, dtype=np.float32), (P, UT, 1))
    return {"ident_rot": id_rot, "cos": np.cos(angle, dtype=np.float32), "sin": np.sin(angle, dtype=np.float32), "rank": rank}


def kernel(**inputs):
    import numpy as _np
    import concourse.bacc as _bacc
    from concourse import mybir as _mybir
    from concourse.bass_utils import run_bass_kernel_spmd as _run

    nc = _bacc.Bacc("TRN2", target_bir_lowering=False, num_devices=1)
    arrays, args = {}, []
    for name in _INS:
        arrays[f"in_{name}"] = _np.ascontiguousarray(inputs[name])
    for name, a in _constants().items():
        arrays[f"const_{name}"] = _np.ascontiguousarray(a)
    for name, a in arrays.items():
        args.append(nc.dram_tensor(name, a.shape, _mybir.dt.float32, kind="ExternalInput").ap())
    out = nc.dram_tensor("out_0", (B, N, D), _mybir.dt.float32, kind="ExternalOutput").ap()
    parts = nc.dram_tensor("parts", (2, H, SPLITS, HD, B * N), _mybir.dt.bfloat16).ap()
    heads_t = nc.dram_tensor("heads_t", (GROUPS_C, OR, B * N), _mybir.dt.float32).ap()
    rden_t = nc.dram_tensor("rden_t", (GROUPS_C, B * N), _mybir.dt.float32).ap()
    layer_kernel(nc, *args, out, parts, heads_t, rden_t)
    r = _run(nc, [arrays], core_ids=[0])
    return r.results[0]["out_0"]
```

```python
import concourse.bass as bass
from concourse import mybir
from contextlib import ExitStack

P = 128
B, N, D = 4, 1024, 128
H, HD = 16, 8
E = 8
TILES = B * N // P
TPB = N // P
HALF = 512
UT = HALF // P
HEADS = B * H
SCALE = float(HD) ** -0.5
EPS = 1e-5
OR = HD + 1
CG = 32

Q_PARTS = [0, 1, 2, 0, 1, 0]
K_PARTS = [0, 0, 0, 1, 1, 2]
SPLITS = 3
PAIR = 2
SROWS = len(Q_PARTS) * PAIR * HD
BLOCK_AT = [K_PARTS.index(s) * PAIR * HD for s in range(SPLITS)]

GROUPS_C = P // HD
HALF_R = HALF // GROUPS_C
BLOCK = N // GROUPS_C

QH = 4
QUADS = HEADS // QH
STEPS = 32
LAG_S = 12
LUMP = 2
S_OFF = STEPS + LAG_S
V_OFF = S_OFF + LUMP + 1
T_MAX = STEPS + 3
T_DEN = V_OFF + STEPS + 8
SLOTS = 8
T_PROJ, T_ROOT, T_Z, T_GATES = 16, 22, 28, 31
EV = E // 2


def layer_kernel(nc, x, qkv_w, qkv_b, proj_w, proj_b, gate_w, expert_w, ident_rot_c, cos_c, sin_c, rank_c, mine_c, out, parts, max_rows, heads_t, rden_t):
    f32, bf16 = mybir.dt.float32, mybir.dt.bfloat16
    ALU, ACT, AX = mybir.AluOpType, mybir.ActivationFunctionType, mybir.AxisListType

    ctx = ExitStack()
    with ctx:
        def sb(name, shape, dt=f32):
            return ctx.enter_context(nc.sbuf_tensor(name, shape, dt))

        def pb(name, shape, dt=f32):
            return ctx.enter_context(nc.psum_tensor(name, shape, dt))

        def sem(name):
            return ctx.enter_context(nc.semaphore(name))

        x_sb = sb("x_sb", [P, TILES, D])
        v_all = sb("v_all", [P, TILES, D])
        ident_rot = sb("ident_rot", [P, 2, P])
        ident = ident_rot[:, 0, :]
        ident_bf = sb("ident_bf", [P, P], bf16)
        cos_t = sb("cos_t", [P, N])
        sin_t = sb("sin_t", [P, N])
        w_nat = sb("w_nat", [P, 3, D])
        w_t = sb("w_t", [P, 5, P])
        b_cols = sb("b_cols", [P, 2])
        b_qk = sb("b_qk", [P, 2, 2])
        vb_row = sb("vb_row", [P, D])
        pb_row = sb("pb_row", [P, D])
        pw_nat = sb("pw_nat", [P, D])
        pw_t = sb("pw_t", [P, D])
        gw_nat = sb("gw_nat", [E, D])
        gw_t = sb("gw_t", [P, E])
        ew_nat = sb("ew_nat", [P, E, D])
        ew_t = sb("ew_t", [P, E, D])
        rank = sb("rank", [P, UT, E])
        eps_c = sb("eps_c", [P, 1])
        credit = sb("credit", [P, 6])
        bn6 = sb("bn6", [P, TILES, 6])
        mv = sb("mv", [P, TILES, 2])
        std = sb("std", [P, TILES])
        rstd = sb("rstd", [P, TILES])
        xn = sb("xn", [P, 2, UT, D])
        xn_t = sb("xn_t", [P, 2, HALF])
        rc = sb("rc", [P, 2, 2, HALF])
        rope = sb("rope", [P, 2, HALF])
        res1 = sb("res1", [P, 2, HALF])
        split_sb = sb("split_sb", [P, 2, SPLITS, HALF], bf16)
        mine = sb("mine", [P, PAIR])
        q_in = sb("q_in", [P, 2, N], bf16)
        q_mx = sb("q_mx", [P, 2, 2, PAIR, N], bf16)
        k_mx = sb("k_mx", [P, 2, 2, N], bf16)
        q_sc = sb("q_sc", [P, 2, 2, N], bf16)
        k_sc = sb("k_sc", [P, 2, 2, PAIR, N], bf16)
        prob = sb("prob", [P, SLOTS, 2, HALF])
        v_ring = sb("v_ring", [P, 2, TPB, QH, CG])
        mx = sb("mx", [P, 2, PAIR, 2, TPB, 2])
        mneg = sb("mneg", [P, 2, PAIR, 2, TPB])
        mres = sb("mres", [P, 2, PAIR, 2, TPB])
        zeros = sb("zeros", [P, PAIR, 2, TPB])
        msp = sb("msp", [P, 2, PAIR, SPLITS, 2, TPB], bf16)
        ms_t = sb("ms_t", [QH * SPLITS * TPB, 2, P], bf16)
        o_sb = sb("o_sb", [P, 2, 2, HALF])
        den = sb("den", [QH * GROUPS_C, 2, BLOCK])
        rden = sb("rden", [QH * GROUPS_C, 2, BLOCK])
        a_raw, a_rden = rc[:, 0, :, :], rc[:, 1, :, :]
        a_t = rope
        x1 = res1[:, :, :].rearrange("p g (t d) -> p g t d", d=D)
        z = xn
        z_t = xn_t
        x1z = sb("x1z", [P, 2, UT, D])
        best = sb("best", [P, 2, UT])
        hit = sb("hit", [P, 2, UT, E])
        rnk = sb("rnk", [P, 2, UT, E])
        brnk = sb("brnk", [P, 2, UT])
        onehot = sb("onehot", [P, 2, UT, E])
        bn6t = sb("bn6t", [P, 2, UT, 6])
        mvt = sb("mvt", [P, 2, UT, 2])
        stdt = sb("stdt", [P, 2, UT])
        rstdt = sb("rstdt", [P, 2, UT])

        y_all = prob[:, 0:4, :, :].rearrange("p s a (b d) -> p (s a b) d", d=D)
        sel = prob[:, 4:6, :, :].rearrange("p s a (b d) -> p s (a b) d", d=D)
        sel2 = prob[:, 6:8, :, :].rearrange("p g a (b c d) -> p g (a b) c d", c=2, d=D)

        ps_nat = [pb(f"ps_nat{i}", [P, HALF]) for i in range(2)]
        ps_s = [pb(f"ps_s{i}", [P, 2 * HALF]) for i in range(2)]
        ps_o = pb("ps_o", [P, HALF])
        ps_m = pb("ps_m", [P, HALF])
        banks_mx = [*ps_nat, ps_m]
        ps_mt = ps_m[0:QH * SPLITS * TPB, 0:P // 2].bitcast(bf16)

        s_x0, s_x, s_const, s_wqkv, s_wtail, s_zeros = sem("first_batch_loaded"), sem("x_loaded"), sem("consts_loaded"), sem("qkv_w_loaded"), sem("tail_w_loaded"), sem("unused_rows_set")
        s_idbf, s_rows, s_eps = sem("ident_bf_made"), sem("tail_rows_loaded"), sem("eps_set")
        s_tw_ps, s_tw_sb = sem("tail_w_t_in_psum"), sem("tail_w_t_in_sbuf")
        s_wt_ps, s_wt_sb = sem("w_t_in_psum"), sem("w_t_in_sbuf")
        s_bn, s_mv, s_std, s_rstd = sem("bn_stats"), sem("mean_var"), sem("std"), sem("rstd")
        s_xn, s_xt_ps, s_xt_sb = sem("xn_made"), sem("xn_t_in_psum"), sem("xn_t_in_sbuf")
        s_qk_ps, s_v_ps, s_rc, s_v_sb = sem("qk_in_psum"), sem("v_in_psum"), sem("rotary_products"), sem("v_in_sbuf")
        s_rope, s_hi, s_res, s_mid, s_lo = sem("rope_made"), sem("high_part"), sem("first_residue"), sem("middle_part"), sem("low_part")
        s_parts = [sem("parts_of_q_stored"), sem("parts_of_k_stored")]
        s_qin, s_qpad, s_kpad = sem("q_in_loaded"), sem("q_mx_made"), sem("k_sc_made")
        s_kmx = [sem("k_mx_loaded_even"), sem("k_mx_loaded_odd")]
        s_qsc = [sem("q_sc_loaded_even"), sem("q_sc_loaded_odd")]
        s_nat, s_mx, s_neg, s_mh, s_mr, s_mm, s_msp = sem("max_scores_in_psum"), sem("max_taken"), sem("max_negated"), sem("max_high"), sem("max_residue"), sem("max_middle"), sem("max_split")
        s_mt_ps, s_mt_sb = sem("max_rows_in_psum"), sem("max_rows_in_sbuf")
        s_mdram, s_mrow = sem("max_rows_in_dram"), sem("max_rows_placed")
        s_sc, s_exp, s_pv, s_vr, s_o = sem("scores_in_psum"), sem("exp_done"), sem("lump_done"), sem("v_ring_filled"), sem("half_in_sbuf")
        s_den, s_rd, s_rdst = sem("den_loaded"), sem("den_inverted"), sem("rden_stored")
        s_xb = sem("x_biased")
        t_at = [sem("attn_staged_even"), sem("attn_staged_odd")]
        t_an, t_y_ps = sem("attn_normalised"), sem("proj_in_psum")
        t_x1, t_bn, t_mv, t_std, t_rstd, t_z = sem("x1_made"), sem("t_bn_stats"), sem("t_mean_var"), sem("t_std"), sem("t_rstd"), sem("z_made")
        t_zt_ps, t_zt_sb, t_g_ps = sem("z_t_in_psum"), sem("z_t_in_sbuf"), sem("gate_in_psum")
        t_hit, t_best, t_rnk, t_brnk, t_oh = sem("best_hit"), sem("best_score"), sem("ranked"), sem("best_rank"), sem("onehot_made")
        t_x1z, t_e_ps, t_selV, t_selA = sem("x1_plus_z"), sem("experts_in_psum"), sem("selected_by_vector"), sem("selected_by_scalar")
        t_s4, t_s2, t_s1, t_out = sem("summed_to_4"), sem("summed_to_2"), sem("summed_to_1"), sem("out_made")
        s_ost = [sem("quad_stored_even"), sem("quad_stored_odd")]
        s_out = sem("out_stored")

        out_t = out.rearrange("b (t p) d -> p (b t) d", p=P)
        block = ctx.enter_context(nc.Block())

        def at(t, off, base, it):
            q, u = divmod(t - off, STEPS)
            if isinstance(base, int) and not 0 <= base + q < QUADS:
                return None, 0, 0, 0
            return base + q, q % 2, it + q // 2, u

        def turns(eng, turn, peel=1):
            turn(0, 0, 0, 2 * peel * STEPS)
            with eng.Fori(peel, QUADS // 2) as it:
                turn(it * 2, it, 0, 2 * STEPS)

        def sums_at(rows, g):
            return rows.rearrange("c (j n) -> c j n", j=H)[:, bass.ds((g % (H // QH)) * QH, QH), bass.ds((g // (H // QH)) * BLOCK, BLOCK)]

        def need(eng, semaphore, count):
            if not isinstance(count, int) or count > 0:
                eng.wait_ge(semaphore, count)

        LOADS = SPLITS * 2
        STATS = [(0, TPB), (TPB, TILES)]

        UNITS = TILES // UT

        def units(eng, unit, peel=0):
            for n in range(2 * peel):
                unit(n, n % 2, 2)
            with eng.Fori(peel, UNITS // 2 - 1) as it:
                for g in range(2):
                    unit(it * 2 + g, g, 2)
            unit(UNITS - 2, 0, 1)
            unit(UNITS - 1, 1, 0)

        @block.sync
        def _(sp):
            sp.dma_start(x_sb[:, 0:TPB, :], x[0].rearrange("(t p) d -> p t d", p=P)).then_inc(s_x0, 16)
            sp.dma_start(w_nat[:, :, :], qkv_w.rearrange("(c p) d -> p c d", p=P)).then_inc(s_wqkv, 16)
            sp.dma_start(b_cols[:, :], qkv_b[0:2 * D].rearrange("(c p) -> p c", p=P), allow_slow_non_contiguous=True).then_inc(s_wqkv, 16)
            sp.dma_start(ident_rot[:, :, :], ident_rot_c).then_inc(s_wqkv, 16)
            sp.dma_start(x_sb[:, TPB:TILES, :], x[1:B].rearrange("b (t p) d -> p (b t) d", p=P)).then_inc(s_x, 16)
            sp.dma_start(cos_t[:, :], cos_c).then_inc(s_const, 16)
            sp.dma_start(sin_t[:, :], sin_c).then_inc(s_const, 16)
            sp.dma_start(vb_row[:, :], qkv_b[2 * D:3 * D].rearrange("(a d) -> a d", a=1).broadcast_to((P, D))).then_inc(s_const, 16)
            sp.dma_start(pb_row[:, :], proj_b.rearrange("(a d) -> a d", a=1).broadcast_to((P, D))).then_inc(s_rows, 16)
            sp.dma_start(rank[:, :, :], rank_c).then_inc(s_rows, 16)
            sp.dma_start(mine[:, :], mine_c).then_inc(s_rows, 16)
            sp.dma_start(pw_nat[:, :], proj_w).then_inc(s_wtail, 16)
            sp.dma_start(gw_nat[:, :], gate_w).then_inc(s_wtail, 16)
            sp.dma_start(ew_nat[:, :, :], expert_w.rearrange("e f h -> f e h")).then_inc(s_wtail, 16)

            def park(f):
                for s in range(SPLITS):
                    for qk in range(2):
                        if s == 0:
                            sp.wait_ge(s_hi, f * 2 + qk + 1)
                        elif s == 1:
                            sp.wait_ge(s_mid, f * 2 + qk + 1)
                        else:
                            sp.wait_ge(s_lo, f * 2 + qk + 1)
                        sp.dma_start(parts[qk, s, :, bass.ds(f * HALF, HALF)], split_sb[:, qk, s, :]).then_inc(s_parts[qk], 16)

            def parked(units_done):
                for qk in range(2):
                    sp.wait_ge(s_parts[qk], 16 * SPLITS * (units_done + 1))

            def load_stack(qk, g, to, signal):
                cols = bass.ds((g // (H // QH)) * N, N)
                for s in range(SPLITS):
                    meets = SPLITS - s
                    for pair in range(2):
                        feats = bass.ds(((g % (H // QH)) * 2 + pair) * PAIR * HD, PAIR * HD)
                        src = parts[1, s:s + 1, feats, cols].broadcast_to((meets, PAIR * HD, N)) if qk else parts[0, 0:meets, feats, cols]
                        sp.dma_start(to[BLOCK_AT[s]:BLOCK_AT[s] + meets * PAIR * HD, pair, :], src).then_inc(signal, 16)

            def store_quad(g, par):
                tok = [((g % (H // QH)) * QH + j) * (N // QH) + (g // (H // QH)) * BLOCK for j in range(QH)]
                sp.wait_ge(s_o, g * 2 + 2)
                for j in range(QH):
                    sp.dma_start(heads_t[:, :, bass.ds(tok[j], BLOCK)].rearrange("c o r -> o c r"),
                                 o_sb[j * CG:j * CG + OR, par, :, :].rearrange("o h (c r) -> o (h c) r", r=BLOCK)).then_inc(s_ost[par], 16)

            def load_sums(g, par, k):
                sums = sums_at(heads_t[:, HD, :], g)
                sp.wait_ge(s_ost[par], 16 * QH * (k + 1))
                sp.dma_start(den[:, par, :], sums).then_inc(s_den, 16)

            def store_inverted(g, par):
                sp.dma_start(sums_at(rden_t, g), rden[:, par, :]).then_inc(s_rdst, 16)

            def feed(g, par, k, last=False):
                later = not isinstance(g, int) or g > 1
                if not last:
                    sp.wait_ge(s_qpad, g + 1)
                    load_stack(0, g + 1, q_in, s_qin)
                    need(sp, s_nat, g * STEPS * 2)
                    need(sp, s_kpad, g)
                    load_stack(1, g + 1, k_mx[:, 1 - par, :, :], s_kmx[1 - par])
                need(sp, s_sc, (g - 1) * STEPS)
                load_stack(0, g, q_sc[:, par, :, :], s_qsc[par])
                if later:
                    store_quad(g - 2, par)
                    load_sums(g - 2, par, k - 1)
                    sp.wait_ge(s_rd, g - 1)
                sp.wait_ge(s_mt_sb, g + 1)
                sp.dma_start(max_rows[par], ms_t[:, par, :]).then_inc(s_mdram, 16)
                sp.wait_ge(s_mdram, 16 * (g + 1))
                sp.dma_start(q_sc[SROWS:SROWS + PAIR * SPLITS, par, :, :].rearrange("r a n -> r (a n)"), max_rows[par].rearrange("(r c) q -> r (c q)", r=PAIR * SPLITS)).then_inc(s_mrow, 16)
                if later:
                    store_inverted(g - 2, par)

            for f in range(4):
                park(f)
                if f == 2:
                    parked(2)
                    sp.wait_ge(s_zeros, 1)
                    load_stack(0, 0, q_in, s_qin)
                if f == 3:
                    load_stack(1, 0, k_mx[:, 0, :, :], s_kmx[0])
            with sp.Fori(4, UNITS) as f:
                park(f)
            parked(UNITS)
            for g in range(2):
                feed(g, g, 0)
            with sp.Fori(1, QUADS // 2 - 1) as it:
                for g in range(2):
                    feed(it * 2 + g, g, it)
            for g in range(QUADS - 2, QUADS):
                feed(g, g % 2, QUADS // 2 - 1, g == QUADS - 1)

            def stage(n, g):
                tok = bass.ds(n * HALF, HALF)
                sp.dma_start(a_raw[:, g, :], heads_t[:, 0:HD, tok]).then_inc(t_at[g], 16)
                sp.dma_start(a_rden[:, g, :], rden_t[:, tok].rearrange("c (a n) -> c a n", a=1).broadcast_to((GROUPS_C, HD, HALF))).then_inc(t_at[g], 16)

            sp.wait_ge(s_rdst, 16 * (QUADS - 2))
            for n in range(2):
                stage(n, n)
            store_quad(QUADS - 2, 0)
            load_sums(QUADS - 2, 0, QUADS // 2 - 1)
            sp.wait_ge(s_rd, QUADS - 1)
            store_inverted(QUADS - 2, 0)
            for n in range(2, 4):
                sp.wait_ge(t_an, n - 1)
                stage(n, n % 2)
            store_quad(QUADS - 1, 1)
            load_sums(QUADS - 1, 1, QUADS // 2 - 1)

            def store(n):
                sp.wait_ge(t_out, n + 1)
                sp.dma_start(out_t[:, bass.ds(n * UT, UT), :], y_all[:, bass.ds(n * UT, UT), :]).then_inc(s_out, 16)

            def move(n, g, ahead):
                if isinstance(n, int) and n == 0:
                    return
                if ahead == 2 and not (isinstance(n, int) and n == 1):
                    sp.wait_ge(t_an, n + 1)
                    stage(n + 2, g)
                store(n - 1)
                if isinstance(n, int) and n == 1:
                    sp.wait_ge(s_rd, QUADS)
                    store_inverted(QUADS - 1, 1)
                    sp.wait_ge(s_rdst, 16 * QUADS)
            units(sp, move, 1)
            store(UNITS - 1)
            sp.wait_ge(s_out, 16 * UNITS)

        @block.gpsimd
        def _(pool):
            nc.gpsimd.memset(eps_c[:, :], EPS).then_inc(s_eps, 1)
            for qk in range(2):
                nc.gpsimd.memset(credit[:, qk:qk + 1], 0.0).then_inc(s_parts[qk], 16 * SPLITS)
            nc.gpsimd.memset(credit[:, 4:5], 0.0).then_inc(s_res, 2)
            nc.gpsimd.memset(zeros[:, :, :, :], 0.0)
            nc.gpsimd.memset(v_ring[:, :, :, :, :], 1.0)
            pool.wait_ge(s_wqkv, 48)
            nc.gpsimd.tensor_copy(ident_bf[:, :], ident).then_inc(s_idbf, 1)

            def residues(f, g, ahead):
                for qk in range(2):
                    pool.wait_ge(s_hi, f * 2 + qk + 1)
                    nc.gpsimd.tensor_tensor(res1[:, qk, :], rope[:, qk, :], split_sb[:, qk, 0, :], ALU.subtract).then_inc(s_res, 1)
                for qk in range(2):
                    pool.wait_ge(s_mid, f * 2 + qk + 1)
                    nc.gpsimd.tensor_tensor(split_sb[:, qk, 2, :], res1[:, qk, :], split_sb[:, qk, 1, :], ALU.subtract).then_inc(s_lo, 1)
            units(pool, residues)

            pool.wait_ge(s_v_sb, UNITS + 1)
            pool.wait_ge(s_rows, 48)
            pool.wait_ge(s_xn, UNITS)

            def values(g, p):
                need(pool, s_pv, (g - 1) * (STEPS // LUMP))
                nc.gpsimd.tensor_copy(v_ring[:, p, :, :, 0:HD], v_all[:, bass.ds((g // (H // QH)) * TPB, TPB), bass.ds((g % (H // QH)) * QH * HD, QH * HD)]
                                      .rearrange("p t (j d) -> p t j d", d=HD)).then_inc(s_vr, 1)

            def split_max(g, p):
                pool.wait_ge(s_neg, g + 1)
                need(pool, s_mt_ps, g - 1)
                high, middle, low = [msp[:, p, :, s, :, :] for s in range(SPLITS)]
                nc.gpsimd.tensor_tensor(high, mneg[:, p, :, :, :], zeros[:, :, :, :], ALU.subtract).then_inc(s_mh, 1)
                pool.wait_ge(s_mh, g + 1)
                nc.gpsimd.tensor_tensor(mres[:, p, :, :, :], mneg[:, p, :, :, :], high, ALU.subtract).then_inc(s_mr, 1)
                pool.wait_ge(s_mr, g + 1)
                nc.gpsimd.tensor_tensor(middle, mres[:, p, :, :, :], zeros[:, :, :, :], ALU.subtract).then_inc(s_mm, 1)
                pool.wait_ge(s_mm, g + 1)
                nc.gpsimd.tensor_tensor(low, mres[:, p, :, :, :], middle, ALU.subtract).then_inc(s_msp, 1)

            def only_mine(to, stack):
                for j in range(PAIR):
                    ins = nc.gpsimd.tensor_tensor(to[:, :, j, :], stack, mine[:, j:j + 1].rearrange("p (a b) -> p a b", a=1).broadcast_to((P, 2, N)), ALU.mult)
                return ins

            def quad(g, p, k, last=False):
                pool.wait_ge(s_kmx[p], 16 * LOADS * (k + 1))
                need(pool, s_sc, (g - 1) * STEPS)
                only_mine(k_sc[:, p, :, :, :], k_mx[:, p, :, :]).then_inc(s_kpad, 1)
                if not last:
                    pool.wait_ge(s_qin, 16 * LOADS * (g + 2))
                    need(pool, s_nat, g * STEPS * 2)
                    only_mine(q_mx[:, 1 - p, :, :, :], q_in[:, :, :]).then_inc(s_qpad, 1)
                values(g, p)
                split_max(g, p)

            nc.gpsimd.tensor_tensor(x_sb[:, :, :], x_sb[:, :, :], pb_row[:, :].rearrange("p (a d) -> p a d", a=1).broadcast_to((P, TILES, D)), ALU.add).then_inc(s_xb, 1)
            for p in range(2):
                quad(p, p, 0)
            with pool.Fori(1, QUADS // 2 - 1) as it:
                for p in range(2):
                    quad(it * 2 + p, p, it)
            for p in range(2):
                quad(QUADS - 2 + p, p, QUADS // 2 - 1, p == 1)

            def normalise(n, g):
                pool.wait_ge(t_at[g], 32 * ((n - g) // 2 + 1))
                nc.gpsimd.tensor_tensor(a_t[:, g, :], a_raw[:, g, :], a_rden[:, g, :], ALU.mult).then_inc(t_an, 1)

            def combine(n, g, ahead):
                if ahead == 2:
                    normalise(n + 2, g)
                need(pool, t_out, n - 1)
                for t in range(UT):
                    c = n * UT + t + 1
                    pool.wait_ge(t_selV, c)
                    pool.wait_ge(t_selA, c)
                    nc.gpsimd.tensor_tensor(sel[:, t % 2, 0:4, :], sel[:, t % 2, 0:4, :], sel[:, t % 2, 4:8, :], ALU.add).then_inc(t_s4, 1)
                    pool.wait_ge(t_s4, c)
                    nc.gpsimd.tensor_tensor(sel2[:, g, t, :, :], sel[:, t % 2, 0:2, :], sel[:, t % 2, 2:4, :], ALU.add).then_inc(t_s2, 1)

            normalise(0, 0)
            normalise(1, 1)
            units(pool, combine, 1)

        @block.scalar
        def _(act):
            act.wait_ge(s_eps, 1)

            def roots(c):
                first, end = STATS[c]
                act.wait_ge(s_mv, end)
                nc.scalar.activation(std[:, first:end], mv[:, first:end, 1], ACT.Sqrt, bias=eps_c[:, :]).then_inc(s_std, 1)

            def xt_copy(f, g):
                act.wait_ge(s_xt_ps, f + 1)
                nc.scalar.activation(xn_t[:, g, :], ps_m[:, :], ACT.Copy).then_inc(s_xt_sb, 1)

            def high_middle(f, g, ahead):
                if ahead:
                    xt_copy(f + 1, 1 - g)
                for qk in range(2):
                    act.wait_ge(s_rope, f * 2 + qk + 1)
                    act.wait_ge(s_parts[qk], 16 * SPLITS * (f + 1))
                    nc.scalar.activation(split_sb[:, qk, 0, :], rope[:, qk, :], ACT.Copy).then_inc(s_hi, 1)
                for qk in range(2):
                    act.wait_ge(s_res, f * 2 + qk + 1 + 2)
                    nc.scalar.activation(split_sb[:, qk, 1, :], res1[:, qk, :], ACT.Copy).then_inc(s_mid, 1)
            roots(0)
            xt_copy(0, 0)
            roots(1)
            units(act, high_middle)
            act.wait_ge(s_tw_ps, 1)
            nc.scalar.activation(ew_t[:, :, :].rearrange("p e d -> p (e d)"), ps_s[0][:, :], ACT.Copy)
            nc.scalar.activation(pw_t[:, :], ps_s[1][:, 0:P], ACT.Copy)
            nc.scalar.activation(gw_t[:, :], ps_s[1][:, P:P + E], ACT.Copy).then_inc(s_tw_sb, 1)

            def turn(base, it, start, end):
                for t in range(start, end):
                    g, par, k, u = at(t, V_OFF + 1, base, it)
                    if g is not None and u % (STEPS // 2) == STEPS // 2 - LUMP:
                        half = u // (STEPS // 2)
                        act.wait_ge(s_pv, (g * 2 + half + 1) * (STEPS // 2 // LUMP))
                        need(act, s_ost[par], 16 * QH * k)
                        nc.scalar.activation(o_sb[:, par, half, :], ps_o[:, :], ACT.Copy).then_inc(s_o, 1)
                    g, par, k, u = at(t, S_OFF, base, it)
                    if g is not None:
                        if u % LUMP == 0:
                            need(act, s_pv, g * (STEPS // LUMP) + u // LUMP - SLOTS // LUMP + 1)
                        act.wait_ge(s_sc, g * STEPS + u + 1)
                        nc.scalar.activation(prob[:, u % SLOTS, :, :].rearrange("p a q -> p (a q)"), ps_s[u % 2][:, :], ACT.Exp, scale=SCALE).then_inc(s_exp, 1)
                    g, par, k, u = at(t, T_MAX, base, it)
                    if g is not None and u == 0:
                        act.wait_ge(s_mt_ps, g + 1)
                        need(act, s_mdram, 16 * (g - 1))
                        nc.scalar.activation(ms_t[:, par, :], ps_mt, ACT.Copy).then_inc(s_mt_sb, 1)

            def root(n, g):
                act.wait_ge(t_mv, n * UT + UT)
                nc.scalar.activation(stdt[:, g, :], mvt[:, g, :, 1], ACT.Sqrt, bias=eps_c[:, :]).then_inc(t_std, 1)

            def z_copy(n, g):
                act.wait_ge(t_zt_ps, n + 1)
                nc.scalar.activation(z_t[:, g, :], ps_m[:, :], ACT.Copy).then_inc(t_zt_sb, 1)

            def select(n, g, t):
                act.wait_ge(t_e_ps, n * UT + t + 1)
                act.wait_ge(t_oh, n + 1)
                need(act, t_s2, n * UT + t - 1)
                for e in range(EV, E):
                    ins = nc.scalar.activation(sel[:, t % 2, e, :], ps_s[t % 2][:, e * D:(e + 1) * D], ACT.Copy, scale=onehot[:, g, t, e:e + 1])
                ins.then_inc(t_selA, 1)

            def tail_unit(n, g, ahead):
                for t in range(UT - 1):
                    select(n, g, t)
                if ahead:
                    z_copy(n + 1, 1 - g)
                select(n, g, UT - 1)
                if ahead == 2:
                    root(n + 2, g)

            turns(act, turn)
            turn(QUADS, QUADS // 2, 0, T_ROOT)
            root(0, 0)
            turn(QUADS, QUADS // 2, T_ROOT, T_Z + 1)
            z_copy(0, 0)
            turn(QUADS, QUADS // 2, T_Z + 1, T_DEN + 1)
            root(1, 1)
            units(act, tail_unit, 1)

        @block.vector
        def _(dve):
            nc.vector.memset(credit[:, 2:3], 0.0).then_inc(s_rc, 2)
            nc.vector.memset(credit[:, 3:4], 0.0).then_inc(s_v_sb, 1)
            nc.vector.memset(q_in[SROWS:P, :, :], 0.0)
            nc.vector.memset(q_sc[SROWS:P, :, :, :], 0.0)
            nc.vector.memset(k_mx[SROWS:P, :, :, :], 1.0).then_inc(s_zeros, 1)

            def statistics(c):
                first, end = STATS[c]
                dve.wait_ge((s_x0, s_x)[c], 16)
                with dve.Fori(first // UT, end // UT) as it:
                    for t in range(UT):
                        nc.vector.bn_stats(bn6[:, bass.ds(it * UT + t, 1), :].rearrange("p a s -> p (a s)"), x_sb[:, bass.ds(it * UT + t, 1), :].rearrange("p a d -> p (a d)")).then_inc(s_bn, 1)
                dve.wait_ge(s_bn, end)
                for t in range(first, end):
                    nc.vector.bn_aggr(mv[:, t, :], bn6[:, t, :]).then_inc(s_mv, 1)
                dve.wait_ge(s_std, c + 1)
                nc.vector.reciprocal(rstd[:, first:end], std[:, first:end]).then_inc(s_rstd, 1)
                dve.wait_ge(s_rstd, c + 1)

            def normalise(f, g):
                for t in range(UT):
                    c = f * UT + t
                    ins = nc.vector.tensor_scalar(xn[:, g, t, :], x_sb[:, bass.ds(c, 1), :].rearrange("p a d -> p (a d)"),
                                                  mv[:, bass.ds(c, 1), 0:1].rearrange("p a s -> p (a s)"), rstd[:, bass.ds(c, 1)], ALU.subtract, ALU.mult)
                ins.then_inc(s_xn, 1)

            def rotate(f, g, ahead):
                if ahead:
                    normalise(f + 1, 1 - g)
                for qk in range(2):
                    n = f * 2 + qk
                    dve.wait_ge(s_qk_ps, n + 1)
                    for a, table in ((0, cos_t), (1, sin_t)):
                        to = rc[:, qk, a, :] if qk else rc[:, qk, a, :].rearrange("p (c r) -> p r c", r=HALF_R)
                        src, tab = ps_s[qk][:, a * HALF:(a + 1) * HALF], table[:, g * HALF:(g + 1) * HALF]
                        if not qk:
                            src, tab = src.rearrange("p (r c) -> p r c", r=HALF_R), tab.rearrange("p (r c) -> p r c", r=HALF_R)
                        ins = nc.vector.scalar_tensor_tensor(to, src, b_qk[:, a, qk:qk + 1], tab, ALU.add, ALU.mult)
                    ins.then_inc(s_rc, 1)
                    dve.wait_ge(s_rc, n + 1 + 2)
                    dve.wait_ge(s_res, n + 1)
                    nc.vector.tensor_tensor(rope[:, qk, :], rc[:, qk, 0, :], rc[:, qk, 1, :], ALU.add).then_inc(s_rope, 1)
                dve.wait_ge(s_v_ps, f + 1)
                nc.vector.tensor_tensor(v_all[:, bass.ds(f * UT, UT), :], ps_o[:, :].rearrange("p (t d) -> p t d", t=UT),
                                        vb_row[:, :].rearrange("p (a d) -> p a d", a=1).broadcast_to((P, UT, D)), ALU.add).then_inc(s_v_sb, 1)
            statistics(0)
            normalise(0, 0)
            dve.wait_ge(s_wt_ps, 1)
            nc.vector.tensor_copy(w_t[:, 0:4, :].rearrange("p c d -> p (c d)"), ps_nat[0][:, :])
            nc.vector.tensor_copy(w_t[:, 4, :], ps_nat[1][:, 0:P])
            nc.vector.tensor_copy(b_qk[:, :, :].rearrange("p a b -> p (a b)"), ps_nat[1][:, P:P + 4]).then_inc(s_wt_sb, 1)
            statistics(1)
            dve.wait_ge(s_const, 48)
            units(dve, rotate)

            dve.wait_ge(s_rows, 48)
            dve.wait_ge(s_qin, 16 * LOADS)
            for j in range(PAIR):
                ins = nc.vector.tensor_scalar(q_mx[:, 0, :, j, :], q_in[:, :, :], mine[:, j:j + 1], None, ALU.mult)
            ins.then_inc(s_qpad, 1)

            def invert(g, par):
                dve.wait_ge(s_den, 16 * (g + 1))
                need(dve, s_rdst, 16 * (g - 1))
                nc.vector.reciprocal(rden[:, par, :], den[:, par, :]).then_inc(s_rd, 1)

            def turn(base, it, start, end):
                for t in range(start, end):
                    g, par, k, u = at(t, 0, base, it)
                    if g is not None:
                        if u == 0:
                            need(dve, s_neg, g - 1)
                        pair, half, tile = u % 2, u // 2 % 2, u // 4
                        for j in range(2):
                            n = u * 2 + j
                            dve.wait_ge(s_nat, g * STEPS * 2 + n + 1)
                            nc.vector.tensor_reduce(mx[:, par, j, pair, tile, half:half + 1], banks_mx[n % 3][:, :], AX.X, ALU.max).then_inc(s_mx, 1)
                        if u == STEPS - 1:
                            dve.wait_ge(s_mx, (g + 1) * STEPS * 2)
                            need(dve, s_msp, g - 1)
                            nc.vector.tensor_reduce(mneg[:, par, :, :, :], mx[:, par, :, :, :, :], AX.X, ALU.max, negate=True).then_inc(s_neg, 1)
                    g, par, k, u = at(t, T_DEN, base, it)
                    if g is not None and u == 0 and not (isinstance(g, int) and g == QUADS - 1):
                        invert(g, par)

            def residual(n, g):
                dve.wait_ge(t_y_ps, n + 1)
                nc.vector.tensor_tensor(x1[:, g, :, :], ps_nat[0][:, :].rearrange("p (t d) -> p t d", t=UT), x_sb[:, bass.ds(n * UT, UT), :], ALU.add).then_inc(t_x1, 1)
                dve.wait_ge(t_x1, n + 1)
                for t in range(UT):
                    nc.vector.bn_stats(bn6t[:, g, t, :], x1[:, g, t, :]).then_inc(t_bn, 1)
                dve.wait_ge(t_bn, n * UT + UT)
                nc.vector.memset(credit[:, 5:6], 0.0)
                for t in range(UT):
                    nc.vector.bn_aggr(mvt[:, g, t, :], bn6t[:, g, t, :]).then_inc(t_mv, 1)

            def second_norm(n, g):
                dve.wait_ge(t_std, n + 1)
                nc.vector.reciprocal(rstdt[:, g, :], stdt[:, g, :]).then_inc(t_rstd, 1)
                dve.wait_ge(t_rstd, n + 1)
                for t in range(UT):
                    ins = nc.vector.tensor_scalar(z[:, g, t, :], x1[:, g, t, :], mvt[:, g, t, 0:1], rstdt[:, g, t:t + 1], ALU.subtract, ALU.mult)
                ins.then_inc(t_z, 1)

            def skip(n, g):
                dve.wait_ge(t_z, n + 1)
                need(dve, t_out, n - 1)
                nc.vector.tensor_tensor(x1z[:, g, :, :], x1[:, g, :, :], z[:, g, :, :], ALU.add).then_inc(t_x1z, 1)

            def choose(n, g):
                gate = ps_m[:, 0:UT * E].rearrange("p (t e) -> p t e", e=E)
                over = (P, UT, E)
                dve.wait_ge(t_g_ps, n + 1)
                nc.vector.tensor_reduce(best[:, g, :], gate, AX.X, ALU.max).then_inc(t_best, 1)
                dve.wait_ge(t_best, n + 1)
                nc.vector.tensor_tensor(hit[:, g, :, :], gate, best[:, g, :].rearrange("p (t a) -> p t a", a=1).broadcast_to(over), ALU.is_equal).then_inc(t_hit, 1)
                dve.wait_ge(t_hit, n + 1)
                nc.vector.tensor_tensor(rnk[:, g, :, :], hit[:, g, :, :], rank[:, :, :], ALU.mult).then_inc(t_rnk, 1)
                dve.wait_ge(t_rnk, n + 1)
                nc.vector.tensor_reduce(brnk[:, g, :], rnk[:, g, :, :], AX.X, ALU.max).then_inc(t_brnk, 1)
                dve.wait_ge(t_brnk, n + 1)
                nc.vector.tensor_tensor(onehot[:, g, :, :], rnk[:, g, :, :], brnk[:, g, :].rearrange("p (t a) -> p t a", a=1).broadcast_to(over), ALU.is_equal).then_inc(t_oh, 1)

            def select(n, g, t):
                dve.wait_ge(t_e_ps, n * UT + t + 1)
                dve.wait_ge(t_oh, n + 1)
                need(dve, t_s2, n * UT + t - 1)
                nc.vector.tensor_tensor(sel[:, t % 2, 0:EV, :], ps_s[t % 2][:, 0:EV * D].rearrange("p (e d) -> p e d", d=D),
                                        onehot[:, g, t, 0:EV].rearrange("p (e a) -> p e a", a=1).broadcast_to((P, EV, D)), ALU.mult).then_inc(t_selV, 1)

            def finish(n, g):
                dve.wait_ge(t_s2, n * UT + UT)
                nc.vector.tensor_tensor(sel2[:, g, :, 0, :], sel2[:, g, :, 0, :], sel2[:, g, :, 1, :], ALU.add).then_inc(t_s1, 1)
                dve.wait_ge(t_s1, n + 1)
                dve.wait_ge(t_x1z, n + 1)
                nc.vector.tensor_tensor(y_all[:, bass.ds(n * UT, UT), :], sel2[:, g, :, 0, :], x1z[:, g, :, :], ALU.add).then_inc(t_out, 1)

            def tail_unit(n, g, ahead):
                if isinstance(n, int) and n == 1:
                    invert(QUADS - 1, 1)
                select(n, g, 0)
                if ahead:
                    second_norm(n + 1, 1 - g)
                select(n, g, 1)
                if not isinstance(n, int) or n > 0:
                    finish(n - 1, 1 - g)
                if ahead:
                    skip(n + 1, 1 - g)
                select(n, g, 2)
                if ahead == 2:
                    residual(n + 2, g)
                select(n, g, 3)
                if ahead:
                    choose(n + 1, 1 - g)

            turns(dve, turn, 2)
            turn(QUADS, QUADS // 2, 0, T_PROJ)
            dve.wait_ge(s_xb, 1)
            residual(0, 0)
            second_norm(0, 0)
            skip(0, 0)
            choose(0, 0)
            residual(1, 1)
            turn(QUADS, QUADS // 2, T_PROJ, T_DEN + 1)
            units(dve, tail_unit, 1)
            finish(UNITS - 1, 1)

        @block.tensor
        def _(pe):
            mm = nc.tensor.matmul
            pe.wait_ge(s_wqkv, 48)
            id_rot = ident_rot[:, :, :].rearrange("p a f -> p (a f)")
            for qk in range(2):
                mm(ps_nat[0][:, qk * 2 * P:(qk + 1) * 2 * P], w_nat[:, qk, :], id_rot, start=True, stop=True)
            mm(ps_nat[1][:, 0:P], w_nat[:, 2, :], ident, start=True, stop=True)
            for a in range(2):
                ins = mm(ps_nat[1][:, P + 2 * a:P + 2 * a + 2], ident_rot[:, a, :], b_cols[:, :], start=True, stop=True)
            ins.then_inc(s_wt_ps, 1)

            def tokens_t(f, g):
                pe.wait_ge(s_xn, f + 1)
                for t in range(UT):
                    ins = nc.tensor.transpose(ps_m[:, t * P:(t + 1) * P], xn[:, g, t, :], ident)
                ins.then_inc(s_xt_ps, 1)

            def project(f, g, ahead):
                pe.wait_ge(s_xt_sb, f + 1)
                for qk in range(2):
                    pe.wait_ge(s_rc, f * 2 + qk + 1)
                    for a in range(2):
                        ins = mm(ps_s[qk][:, a * HALF:(a + 1) * HALF], w_t[:, 2 * qk + a, :], xn_t[:, g, :], start=True, stop=True)
                    ins.then_inc(s_qk_ps, 1)
                    if ahead and qk == 0:
                        tokens_t(f + 1, 1 - g)
                pe.wait_ge(s_v_sb, f + 1)
                for t in range(UT):
                    ins = mm(ps_o[:, t * P:(t + 1) * P], xn_t[:, g, t * P:(t + 1) * P], w_t[:, 4, :], start=True, stop=True)
                ins.then_inc(s_v_ps, 1)
            tokens_t(0, 0)
            pe.wait_ge(s_wt_sb, 1)
            units(pe, project)
            pe.wait_ge(s_rc, 2 * UNITS + 2)
            pe.wait_ge(s_v_sb, UNITS + 1)
            pe.wait_ge(s_idbf, 1)

            pe.wait_ge(s_wtail, 48)
            for e in range(E):
                nc.tensor.transpose(ps_s[0][:, e * P:(e + 1) * P], ew_nat[:, e, :], ident)
            nc.tensor.transpose(ps_s[1][:, 0:P], pw_nat[:, :], ident)
            nc.tensor.transpose(ps_s[1][:, P:P + E], gw_nat[:, :], ident_rot[0:E, 0, 0:E]).then_inc(s_tw_ps, 1)

            MAX_ROWS_AFTER = (T_MAX - STEPS) * 2 - 1
            q_by_c = q_sc[:, :, :, :].rearrange("p g a (u c r) -> p g a c u r", u=2, r=HALF_R)

            def turn(base, it, start, end):
                for t in range(start, end):
                    g, par, k, u = at(t, S_OFF, base, it)
                    if g is not None:
                        pair, tile, half = u % 2, u // 2 % TPB, u // (2 * TPB)
                        if u == 0:
                            pe.wait_ge(s_qsc[par], 16 * LOADS * (k + 1))
                            pe.wait_ge(s_kpad, g + 1)
                            pe.wait_ge(s_mrow, 16 * (g + 1))
                            if isinstance(g, int) and g == 0:
                                pe.wait_ge(s_tw_sb, 1)
                        need(pe, s_exp, g * STEPS + u - 1)
                        for j in range(2):
                            ins = mm(ps_s[u % 2][:, j * HALF:(j + 1) * HALF], k_sc[:, par, pair, j, tile * P:(tile + 1) * P],
                                     q_by_c[:, par, pair, half * 8:(half + 1) * 8, :, :], start=True, stop=True)
                        ins.then_inc(s_sc, 1)
                    g, par, k, u = at(t, 0, base, it)
                    if g is not None:
                        pair, half, tile = u % 2, u // 2 % 2, u // 4
                        if u == 0:
                            pe.wait_ge(s_kmx[par], 16 * LOADS * (k + 1))
                            pe.wait_ge(s_qpad, g + 1)
                        for j in range(2):
                            n = u * 2 + j
                            before = n - 3 if n >= 3 else (-1, -3, -2)[n]
                            need(pe, s_mx, g * STEPS * 2 + before + 1)
                            if n == MAX_ROWS_AFTER + 3:
                                need(pe, s_mt_sb, g)
                            mm(banks_mx[n % 3][:, :], q_mx[:, par, pair, j, tile * P:(tile + 1) * P], k_mx[:, par, pair, half * HALF:(half + 1) * HALF],
                               start=True, stop=True).then_inc(s_nat, 1)
                    g, par, k, u = at(t, V_OFF, base, it)
                    if g is not None and u % LUMP == 0:
                        half = u // (STEPS // 2)
                        if u == 0:
                            pe.wait_ge(s_vr, g + 1)
                        if u % (STEPS // 2) == 0:
                            need(pe, s_o, g * 2 + half)
                        pe.wait_ge(s_exp, g * STEPS + u + LUMP)
                        for n in range(0, LUMP, 2):
                            tile, slot = (u + n) // 2 % TPB, (u + n) % SLOTS
                            for j in range(QH):
                                ins = mm(ps_o[j * CG:(j + 1) * CG, :], v_ring[:, par, tile, j, :], prob[:, slot + j // 2, j % 2, :],
                                         start=tile == 0, stop=tile == TPB - 1)
                        ins.then_inc(s_pv, 1)
                    g, par, k, u = at(t, T_MAX, base, it)
                    if g is not None and u == 0:
                        pe.wait_ge(s_msp, g + 1)
                        if not (isinstance(g, int) and g == QUADS - 1):
                            pe.wait_ge(s_mx, (g + 1) * STEPS * 2 + MAX_ROWS_AFTER + 1)
                        nc.tensor.transpose(ps_mt, msp[:, par, :, :, :, :].rearrange("p j s a t -> p (j s a t)"), ident_bf[:, :]).then_inc(s_mt_ps, 1)

            def attn_proj(n, g):
                pe.wait_ge(t_an, n + 1)
                need(pe, t_x1, n)
                for t in range(UT):
                    ins = mm(ps_nat[0][:, t * P:(t + 1) * P], a_t[:, g, t * P:(t + 1) * P], pw_t[:, :], start=True, stop=True)
                ins.then_inc(t_y_ps, 1)

            def z_transpose(n, g):
                pe.wait_ge(t_z, n + 1)
                need(pe, t_oh, n)
                for t in range(UT):
                    ins = nc.tensor.transpose(ps_m[:, t * P:(t + 1) * P], z[:, g, t, :], ident)
                ins.then_inc(t_zt_ps, 1)

            def gates(n, g):
                pe.wait_ge(t_zt_sb, n + 1)
                for t in range(UT):
                    ins = mm(ps_m[:, t * E:(t + 1) * E], z_t[:, g, t * P:(t + 1) * P], gw_t[:, :], start=True, stop=True)
                ins.then_inc(t_g_ps, 1)

            def experts(n, g, t):
                need(pe, t_selV, n * UT + t - 1)
                need(pe, t_selA, n * UT + t - 1)
                for half in range(2):
                    ins = mm(ps_s[t % 2][:, half * HALF:(half + 1) * HALF], z_t[:, g, t * P:(t + 1) * P],
                             ew_t[:, half * 4:(half + 1) * 4, :].rearrange("p e d -> p (e d)"), start=True, stop=True)
                ins.then_inc(t_e_ps, 1)

            def tail_unit(n, g, ahead):
                for t in range(UT - 1):
                    experts(n, g, t)
                if ahead:
                    z_transpose(n + 1, 1 - g)
                if ahead == 2:
                    attn_proj(n + 2, g)
                experts(n, g, UT - 1)
                if ahead:
                    gates(n + 1, 1 - g)

            turns(pe, turn)
            turn(QUADS, QUADS // 2, 0, T_PROJ)
            attn_proj(0, 0)
            turn(QUADS, QUADS // 2, T_PROJ, T_Z)
            z_transpose(0, 0)
            attn_proj(1, 1)
            turn(QUADS, QUADS // 2, T_Z, T_GATES)
            gates(0, 0)
            turn(QUADS, QUADS // 2, T_GATES, T_DEN + 1)
            units(pe, tail_unit, 1)


_INS = ["L0_attn_x", "L0_attn_qkv_w", "L0_attn_qkv_b", "L0_attn_proj_w", "L0_attn_proj_b", "L0_ffn_gate_w", "L0_ffn_expert_w"]


def _constants():
    import numpy as np
    f = np.arange(P)
    id_rot = np.zeros((P, 2, P), np.float32)
    id_rot[f, 0, f] = 1.0
    low = f % HD < HD // 2
    id_rot[np.where(low, f + HD // 2, f - HD // 2), 1, f] = np.where(low, -1.0, 1.0)
    inv_freq = (np.float32(1.0) / np.float32(10000.0) ** (np.arange(0, HD, 2, dtype=np.float32) / np.float32(HD))).astype(np.float32)
    angle = np.arange(N, dtype=np.float32)[None, :] * inv_freq[f % (HD // 2)][:, None]
    rank = np.tile(np.arange(E, 0, -1, dtype=np.float32), (P, UT, 1))
    r = np.arange(SROWS + PAIR * SPLITS)
    whose = np.where(r < SROWS, r // HD % PAIR, (r - SROWS) // SPLITS)
    mine = np.zeros((P, PAIR), np.float32)
    mine[r, whose] = 1.0
    return {"ident_rot": id_rot, "cos": np.cos(angle, dtype=np.float32), "sin": np.sin(angle, dtype=np.float32), "rank": rank, "mine": mine}


def kernel(**inputs):
    import numpy as _np
    import concourse.bacc as _bacc
    from concourse import mybir as _mybir
    from concourse.bass_utils import run_bass_kernel_spmd as _run

    nc = _bacc.Bacc("TRN2", target_bir_lowering=False, num_devices=1)
    arrays, args = {}, []
    for name in _INS:
        arrays[f"in_{name}"] = _np.ascontiguousarray(inputs[name])
    for name, a in _constants().items():
        arrays[f"const_{name}"] = _np.ascontiguousarray(a)
    for name, a in arrays.items():
        args.append(nc.dram_tensor(name, a.shape, _mybir.dt.float32, kind="ExternalInput").ap())
    out = nc.dram_tensor("out_0", (B, N, D), _mybir.dt.float32, kind="ExternalOutput").ap()
    parts = nc.dram_tensor("parts", (2, SPLITS, D, B * N), _mybir.dt.bfloat16).ap()
    max_rows = nc.dram_tensor("max_rows", (2, QH * SPLITS * TPB, P), _mybir.dt.bfloat16).ap()
    heads_t = nc.dram_tensor("heads_t", (GROUPS_C, OR, B * N), _mybir.dt.float32).ap()
    rden_t = nc.dram_tensor("rden_t", (GROUPS_C, B * N), _mybir.dt.float32).ap()
    layer_kernel(nc, *args, out, parts, max_rows, heads_t, rden_t)
    r = _run(nc, [arrays], core_ids=[0])
    return r.results[0]["out_0"]
```
